# Optimizing a Trainium2 kernel written in Bass

```python
import numpy as np
import jax
import jax.numpy as jnp

def _softmax(x, axis=-1):
    return jax.nn.softmax(x, axis=axis)

def _gelu(x):
    return jax.nn.gelu(x, approximate=True)

def _silu(x):
    return jax.nn.silu(x)

def _sigmoid(x):
    return jax.nn.sigmoid(x)

def _layernorm(x, axis=-1, eps=1e-05):
    m = jnp.mean(x, axis=axis, keepdims=True)
    v = jnp.var(x, axis=axis, keepdims=True)
    return (x - m) / jnp.sqrt(v + eps)

def _scatter_add(tgt, idx, src, axis=0):
    return tgt.at[idx].add(src)

def _segment_sum(src, seg, n):
    return jax.ops.segment_sum(src, seg, n)
kernel_name = 'mk_seq_preln_d2_jaxref_r8_a987fd'

def setup_inputs(seed: int=0):
    np.random.seed(seed)
    _w = jnp.asarray

    def _L0_attn_setup():
        import jax, jax.numpy as jnp
        import numpy as np
        H = 128
        NH = 32
        D = H // NH
        M = 2
        BMIN, BMAX = (0.85, 0.9995)
        EPS = 1e-06
        ROPE_BASE = 10000.0
        LN_EPS = 1e-05

        def _rope(u, cos, sin):
            half = D // 2
            u1, u2 = (u[..., :half], u[..., half:])
            return jnp.concatenate([u1 * cos - u2 * sin, u1 * sin + u2 * cos], axis=-1)

        def _forward(x, Wq, Wk, Wv, Wbeta, bbeta, Wmix, bmix, Wout, bout, ln_g, ln_b):
            b, t, _ = x.shape
            q = (x @ Wq.T).reshape(b, t, NH, D)
            k = (x @ Wk.T).reshape(b, t, NH, D)
            v = (x @ Wv.T).reshape(b, t, NH, D)
            half = D // 2
            inv_freq = 1.0 / ROPE_BASE ** (jnp.arange(half, dtype=jnp.float32) / half)
            freqs = jnp.arange(t, dtype=jnp.float32)[:, None] * inv_freq
            cos = jnp.cos(freqs)[None, :, None, :]
            sin = jnp.sin(freqs)[None, :, None, :]
            q = _rope(q, cos, sin)
            k = _rope(k, cos, sin)
            phi_q = jax.nn.elu(q) + 1.0
            phi_k = jax.nn.elu(k) + 1.0
            beta = jnp.clip(jax.nn.sigmoid((x @ Wbeta.T + bbeta).reshape(b, t, NH, M)), BMIN, BMAX)
            mix = jax.nn.softmax((x @ Wmix.T + bmix).reshape(b, t, NH, M), axis=-1)

            def step(carry, xs):
                S, K = carry
                pq, pk, vt, bt, mt = xs
                K = K * bt[..., None] + pk[:, :, None, :]
                S = S * bt[..., None, None] + pk[:, :, None, :, None] * vt[:, :, None, None, :]
                num = jnp.einsum('bhd,bhmdc->bhmc', pq, S)
                den = jnp.einsum('bhd,bhmd->bhm', pq, K) + EPS
                y = jnp.sum(num / den[..., None] * mt[..., None], axis=2)
                return ((S, K), y)
            S0 = jnp.zeros((b, NH, M, D, D), x.dtype)
            K0 = jnp.zeros((b, NH, M, D), x.dtype)
            tf = lambda a: jnp.moveaxis(a, 1, 0)
            _, ys = jax.lax.scan(step, (S0, K0), (tf(phi_q), tf(phi_k), tf(v), tf(beta), tf(mix)))
            y = jnp.moveaxis(ys, 0, 1).reshape(b, t, H) @ Wout.T + bout
            z = x + y
            mu = z.mean(-1, keepdims=True)
            var = ((z - mu) ** 2).mean(-1, keepdims=True)
            return (z - mu) / jnp.sqrt(var + LN_EPS) * ln_g + ln_b
        key = jax.random.key(seed)
        ks = jax.random.split(key, 8)
        b, t = (4, 128)
        x = jax.random.normal(ks[0], (b, t, H), jnp.float32)
        sc = (6.0 / (H + H)) ** 0.5
        Wq = jax.random.uniform(ks[1], (H, H), jnp.float32, -sc, sc)
        Wk = jax.random.uniform(ks[2], (H, H), jnp.float32, -sc, sc)
        Wv = jax.random.uniform(ks[3], (H, H), jnp.float32, -sc, sc)
        Wout = jax.random.uniform(ks[4], (H, H), jnp.float32, -sc, sc)
        bout = jnp.zeros((H,), jnp.float32)
        scb = (6.0 / (H + NH * M)) ** 0.5
        Wbeta = jax.random.uniform(ks[5], (NH * M, H), jnp.float32, -scb, scb)
        targets = jnp.linspace(BMIN, BMAX, M)
        bbeta = jnp.tile(jnp.log(targets / (1.0 - targets)), NH)
        Wmix = jnp.zeros((NH * M, H), jnp.float32)
        bmix = jnp.zeros((NH * M,), jnp.float32)
        ln_g = jnp.ones((H,), jnp.float32)
        ln_b = jnp.zeros((H,), jnp.float32)
        return dict(x=x, Wq=Wq, Wk=Wk, Wv=Wv, Wbeta=Wbeta, bbeta=bbeta, Wmix=Wmix, bmix=bmix, Wout=Wout, bout=bout, ln_g=ln_g, ln_b=ln_b)
    _L0_attn_in = _L0_attn_setup()

    def _L0_ffn_setup():
        import jax, jax.numpy as jnp
        import numpy as np
        E = 8
        TOP_K = 2
        CAP_FACTOR = 1.25
        MIN_CAP = 4
        SCORE_SCALE = 1.0

        def _ffn(x, w1, b1, w2, b2):
            return jax.nn.gelu(x @ w1 + b1, approximate=False) @ w2 + b2
        key = jax.random.key(seed)
        ks = jax.random.split(key, 6)
        B, S, D, I = (4, 256, 128, 512)
        std = 0.02
        return {'x': jax.random.normal(ks[0], (B, S, D), jnp.float32), 'Wr': jax.random.normal(ks[1], (E, D), jnp.float32) * std, 'W1': jax.random.normal(ks[2], (E, D, I), jnp.float32) * std, 'b1': jnp.zeros((E, I), jnp.float32), 'W2': jax.random.normal(ks[3], (E, I, D), jnp.float32) * std, 'b2': jnp.zeros((E, D), jnp.float32), 'fw1': jax.random.normal(ks[4], (D, I), jnp.float32) * std, 'fb1': jnp.zeros((I,), jnp.float32), 'fw2': jax.random.normal(ks[5], (I, D), jnp.float32) * std, 'fb2': jnp.zeros((D,), jnp.float32)}
    _L0_ffn_in = _L0_ffn_setup()

    def _L1_attn_setup():
        import jax, jax.numpy as jnp
        import numpy as np
        D_MODEL = 128
        NHEAD = 16
        HEAD_DIM = D_MODEL // NHEAD
        B, L = (4, 1024)
        LN_EPS = 1e-05

        def _decay_scan(v, lam):
            a = jnp.broadcast_to(lam[None, None, :, None], v.shape)

            def combine(c1, c2):
                a1, b1 = c1
                a2, b2 = c2
                return (a1 * a2, b1 * a2 + b2)
            _, state = jax.lax.associative_scan(combine, (a, v), axis=1)
            return state

        def _layernorm(y, gamma, beta):
            mu = jnp.mean(y, axis=-1, keepdims=True)
            var = jnp.mean(jnp.square(y - mu), axis=-1, keepdims=True)
            return (y - mu) * jax.lax.rsqrt(var + LN_EPS) * gamma + beta
        key = jax.random.key(seed)
        ks = jax.random.split(key, 8)
        s = 1.0 / np.sqrt(D_MODEL)
        return {'x': jax.random.normal(ks[0], (B, L, D_MODEL), dtype=jnp.float32), 'decay': jax.random.uniform(ks[1], (NHEAD,), dtype=jnp.float32, minval=0.8, maxval=0.999), 'Wq': jax.random.normal(ks[2], (D_MODEL, D_MODEL), dtype=jnp.float32) * s, 'Wv': jax.random.normal(ks[3], (D_MODEL, D_MODEL), dtype=jnp.float32) * s, 'Wg': jax.random.normal(ks[4], (D_MODEL, D_MODEL), dtype=jnp.float32) * s, 'Wo': jax.random.normal(ks[5], (D_MODEL, D_MODEL), dtype=jnp.float32) * s, 'ln_gamma': jnp.ones((D_MODEL,), dtype=jnp.float32), 'ln_beta': jnp.zeros((D_MODEL,), dtype=jnp.float32)}
    _L1_attn_in = _L1_attn_setup()

    def _L1_ffn_setup():
        import jax, jax.numpy as jnp
        import numpy as np
        DIM = 128
        DEPTH = 2
        HEADS = 8
        DIM_HEAD = 64
        WINDOW = 64
        INNER = HEADS * DIM_HEAD
        HID = int(DIM * 4 * 2 / 3)
        B, N = (2, 1024)
        QK_SCALE = 8.0

        def shift_token(t):
            t1, t2 = jnp.split(t, 2, axis=-1)
            t2 = jnp.pad(t2, ((0, 0), (1, 0), (0, 0)))[:, :-1]
            return jnp.concatenate([t1, t2], axis=-1)

        def l2norm(t):
            return t / jnp.clip(jnp.linalg.norm(t, axis=-1, keepdims=True), 1e-12)

        def rotate_half(x):
            x1, x2 = jnp.split(x, 2, axis=-1)
            return jnp.concatenate([-x2, x1], axis=-1)

        def rotary_xpos(q, k):
            n = q.shape[-2]
            half_idx = jnp.arange(0, DIM_HEAD, 2, dtype=jnp.float32)
            inv_freq = 1.0 / 10000.0 ** (half_idx / DIM_HEAD)
            t = jnp.arange(n, dtype=jnp.float32)
            freqs = t[:, None] * inv_freq[None, :]
            freqs = jnp.concatenate([freqs, freqs], axis=-1)
            base = (half_idx + 0.4 * DIM_HEAD) / (1.4 * DIM_HEAD)
            power = (t - n // 2) / float(WINDOW // 2)
            scale = base[None, :] ** power[:, None]
            scale = jnp.concatenate([scale, scale], axis=-1)
            cos, sin = (jnp.cos(freqs), jnp.sin(freqs))
            q = q * cos * scale + rotate_half(q) * sin * scale
            k = k * cos / scale + rotate_half(k) * sin / scale
            return (q, k)

        def local_attention(q, k, v):
            b, h, n, d = q.shape
            w = n // WINDOW
            bq = q.reshape(b, h, w, WINDOW, d) * QK_SCALE
            bk = k.reshape(b, h, w, WINDOW, d)
            bv = v.reshape(b, h, w, WINDOW, d)

            def look_around(t):
                p = jnp.pad(t, ((0, 0), (0, 0), (1, 0), (0, 0), (0, 0)))
                return jnp.concatenate([p[:, :, :w], p[:, :, 1:]], axis=3)
            bk, bv = (look_around(bk), look_around(bv))
            bt = jnp.arange(n).reshape(w, WINDOW)
            btp = jnp.pad(bt, ((1, 0), (0, 0)), constant_values=-1)
            btk = jnp.concatenate([btp[:w], btp[1:]], axis=1)
            sim = jnp.einsum('bhwid,bhwjd->bhwij', bq, bk)
            i = bt[:, :, None]
            j = btk[:, None, :]
            mask = (i < j) | (i > j + WINDOW) | (j == -1)
            sim = jnp.where(mask, -jnp.finfo(sim.dtype).max, sim)
            attn = jax.nn.softmax(sim, axis=-1)
            out = jnp.einsum('bhwij,bhwjd->bhwid', attn, bv)
            return out.reshape(b, h, n, d)

        def _layer(x, wqkv, qs, ksc, wo, lg, lb, w1, b1, w2, b2):
            b, n, _ = x.shape
            h = shift_token(x)
            qkv = h @ wqkv
            q, k, v = jnp.split(qkv, 3, axis=-1)
            to_heads = lambda t: t.reshape(b, n, HEADS, DIM_HEAD).transpose(0, 2, 1, 3)
            q, k, v = (to_heads(q), to_heads(k), to_heads(v))
            q = l2norm(q) * qs
            k = l2norm(k) * ksc
            q, k = rotary_xpos(q, k)
            o = local_attention(q, k, v)
            o = o.transpose(0, 2, 1, 3).reshape(b, n, INNER)
            x = x + o @ wo
            h = shift_token(x)
            mu = h.mean(-1, keepdims=True)
            var = h.var(-1, keepdims=True)
            h = (h - mu) / jnp.sqrt(var + 1e-05) * lg + lb
            h = h @ w1 + b1
            a, g = jnp.split(h, 2, axis=-1)
            h = a * jax.nn.gelu(g, approximate=False)
            x = x + h @ w2 + b2
            return x
        key = jax.random.key(seed)
        ks = jax.random.split(key, 6)
        return {'x': jax.random.normal(ks[0], (B, N, DIM), jnp.float32), 'wqkv': jax.random.normal(ks[1], (DEPTH, DIM, 3 * INNER), jnp.float32) * 0.02, 'q_scale': jnp.ones((DEPTH, DIM_HEAD), jnp.float32), 'k_scale': jnp.ones((DEPTH, DIM_HEAD), jnp.float32), 'wo': jax.random.normal(ks[2], (DEPTH, INNER, DIM), jnp.float32) * 0.02, 'ln_g': jnp.ones((DEPTH, DIM), jnp.float32), 'ln_b': jnp.zeros((DEPTH, DIM), jnp.float32), 'w1': jax.random.normal(ks[3], (DEPTH, DIM, 2 * HID), jnp.float32) * 0.02, 'b1': jnp.zeros((DEPTH, 2 * HID), jnp.float32), 'w2': jax.random.normal(ks[4], (DEPTH, HID, DIM), jnp.float32) * 0.02, 'b2': jnp.zeros((DEPTH, DIM), jnp.float32)}
    _L1_ffn_in = _L1_ffn_setup()
    _d = {'L0_attn_x': _L0_attn_in['x'], 'L0_attn_Wq': _L0_attn_in['Wq'], 'L0_attn_Wk': _L0_attn_in['Wk'], 'L0_attn_Wv': _L0_attn_in['Wv'], 'L0_attn_Wbeta': _L0_attn_in['Wbeta'], 'L0_attn_bbeta': _L0_attn_in['bbeta'], 'L0_attn_Wmix': _L0_attn_in['Wmix'], 'L0_attn_bmix': _L0_attn_in['bmix'], 'L0_attn_Wout': _L0_attn_in['Wout'], 'L0_attn_bout': _L0_attn_in['bout'], 'L0_attn_ln_g': _L0_attn_in['ln_g'], 'L0_attn_ln_b': _L0_attn_in['ln_b'], 'L0_ffn_Wr': _L0_ffn_in['Wr'], 'L0_ffn_W1': _L0_ffn_in['W1'], 'L0_ffn_b1': _L0_ffn_in['b1'], 'L0_ffn_W2': _L0_ffn_in['W2'], 'L0_ffn_b2': _L0_ffn_in['b2'], 'L0_ffn_fw1': _L0_ffn_in['fw1'], 'L0_ffn_fb1': _L0_ffn_in['fb1'], 'L0_ffn_fw2': _L0_ffn_in['fw2'], 'L0_ffn_fb2': _L0_ffn_in['fb2'], 'L1_attn_decay': _L1_attn_in['decay'], 'L1_attn_Wq': _L1_attn_in['Wq'], 'L1_attn_Wv': _L1_attn_in['Wv'], 'L1_attn_Wg': _L1_attn_in['Wg'], 'L1_attn_Wo': _L1_attn_in['Wo'], 'L1_attn_ln_gamma': _L1_attn_in['ln_gamma'], 'L1_attn_ln_beta': _L1_attn_in['ln_beta'], 'L1_ffn_wqkv': _L1_ffn_in['wqkv'], 'L1_ffn_q_scale': _L1_ffn_in['q_scale'], 'L1_ffn_k_scale': _L1_ffn_in['k_scale'], 'L1_ffn_wo': _L1_ffn_in['wo'], 'L1_ffn_ln_g': _L1_ffn_in['ln_g'], 'L1_ffn_ln_b': _L1_ffn_in['ln_b'], 'L1_ffn_w1': _L1_ffn_in['w1'], 'L1_ffn_b1': _L1_ffn_in['b1'], 'L1_ffn_w2': _L1_ffn_in['w2'], 'L1_ffn_b2': _L1_ffn_in['b2']}
    _x0 = _d['L0_attn_x']
    _d['L0_attn_x'] = jax.random.normal(jax.random.fold_in(jax.random.key(seed), 1), (16, 256, 128), dtype=_x0.dtype)
    del _x0
    return _d

def reference(L0_attn_x, L0_attn_Wq, L0_attn_Wk, L0_attn_Wv, L0_attn_Wbeta, L0_attn_bbeta, L0_attn_Wmix, L0_attn_bmix, L0_attn_Wout, L0_attn_bout, L0_attn_ln_g, L0_attn_ln_b, L0_ffn_Wr, L0_ffn_W1, L0_ffn_b1, L0_ffn_W2, L0_ffn_b2, L0_ffn_fw1, L0_ffn_fb1, L0_ffn_fw2, L0_ffn_fb2, L1_attn_decay, L1_attn_Wq, L1_attn_Wv, L1_attn_Wg, L1_attn_Wo, L1_attn_ln_gamma, L1_attn_ln_beta, L1_ffn_wqkv, L1_ffn_q_scale, L1_ffn_k_scale, L1_ffn_wo, L1_ffn_ln_g, L1_ffn_ln_b, L1_ffn_w1, L1_ffn_b1, L1_ffn_w2, L1_ffn_b2):

    def _L0_attn_ref(x, Wq, Wk, Wv, Wbeta, bbeta, Wmix, bmix, Wout, bout, ln_g, ln_b):
        import jax, jax.numpy as jnp
        import numpy as np
        H = 128
        NH = 32
        D = H // NH
        M = 2
        BMIN, BMAX = (0.85, 0.9995)
        EPS = 1e-06
        ROPE_BASE = 10000.0
        LN_EPS = 1e-05

        def _rope(u, cos, sin):
            half = D // 2
            u1, u2 = (u[..., :half], u[..., half:])
            return jnp.concatenate([u1 * cos - u2 * sin, u1 * sin + u2 * cos], axis=-1)

        def _forward(x, Wq, Wk, Wv, Wbeta, bbeta, Wmix, bmix, Wout, bout, ln_g, ln_b):
            b, t, _ = x.shape
            q = (x @ Wq.T).reshape(b, t, NH, D)
            k = (x @ Wk.T).reshape(b, t, NH, D)
            v = (x @ Wv.T).reshape(b, t, NH, D)
            half = D // 2
            inv_freq = 1.0 / ROPE_BASE ** (jnp.arange(half, dtype=jnp.float32) / half)
            freqs = jnp.arange(t, dtype=jnp.float32)[:, None] * inv_freq
            cos = jnp.cos(freqs)[None, :, None, :]
            sin = jnp.sin(freqs)[None, :, None, :]
            q = _rope(q, cos, sin)
            k = _rope(k, cos, sin)
            phi_q = jax.nn.elu(q) + 1.0
            phi_k = jax.nn.elu(k) + 1.0
            beta = jnp.clip(jax.nn.sigmoid((x @ Wbeta.T + bbeta).reshape(b, t, NH, M)), BMIN, BMAX)
            mix = jax.nn.softmax((x @ Wmix.T + bmix).reshape(b, t, NH, M), axis=-1)

            def step(carry, xs):
                S, K = carry
                pq, pk, vt, bt, mt = xs
                K = K * bt[..., None] + pk[:, :, None, :]
                S = S * bt[..., None, None] + pk[:, :, None, :, None] * vt[:, :, None, None, :]
                num = jnp.einsum('bhd,bhmdc->bhmc', pq, S)
                den = jnp.einsum('bhd,bhmd->bhm', pq, K) + EPS
                y = jnp.sum(num / den[..., None] * mt[..., None], axis=2)
                return ((S, K), y)
            S0 = jnp.zeros((b, NH, M, D, D), x.dtype)
            K0 = jnp.zeros((b, NH, M, D), x.dtype)
            tf = lambda a: jnp.moveaxis(a, 1, 0)
            _, ys = jax.lax.scan(step, (S0, K0), (tf(phi_q), tf(phi_k), tf(v), tf(beta), tf(mix)))
            y = jnp.moveaxis(ys, 0, 1).reshape(b, t, H) @ Wout.T + bout
            z = x + y
            mu = z.mean(-1, keepdims=True)
            var = ((z - mu) ** 2).mean(-1, keepdims=True)
            return (z - mu) / jnp.sqrt(var + LN_EPS) * ln_g + ln_b
        return _forward(x, Wq, Wk, Wv, Wbeta, bbeta, Wmix, bmix, Wout, bout, ln_g, ln_b)

    def _L0_ffn_ref(x, Wr, W1, b1, W2, b2, fw1, fb1, fw2, fb2):
        import jax, jax.numpy as jnp
        import numpy as np
        E = 8
        TOP_K = 2
        CAP_FACTOR = 1.25
        MIN_CAP = 4
        SCORE_SCALE = 1.0

        def _ffn(x, w1, b1, w2, b2):
            return jax.nn.gelu(x @ w1 + b1, approximate=False) @ w2 + b2
        B, S, D = x.shape
        T = B * S
        x_flat = x.reshape(T, D)
        logits = x_flat @ Wr.T * SCORE_SCALE
        probs = jax.nn.softmax(logits, axis=-1)
        topk_scores, topk_experts = jax.lax.top_k(probs, TOP_K)
        topk_scores = topk_scores / jnp.clip(topk_scores.sum(-1, keepdims=True), 1e-09, None)
        cap = max(int(CAP_FACTOR * (T * TOP_K / E)), MIN_CAP)
        y_fb = _ffn(x_flat, fw1, fb1, fw2, fb2)
        y_flat = jnp.zeros_like(x_flat)
        fallback = jnp.zeros((T,), bool)
        tok_ids = jnp.arange(T, dtype=jnp.int32)
        for e in range(E):
            match = topk_experts == e
            elig = match.any(-1) & ~fallback
            pos = jnp.cumsum(elig) - 1
            kept = elig & (pos < cap)
            overflow = elig & (pos >= cap)
            slot = jnp.where(kept, pos, cap)
            buf = jnp.zeros((cap + 1,), jnp.int32).at[slot].set(tok_ids)
            vmask = jnp.zeros((cap + 1,), bool).at[slot].set(kept)
            idx = buf[:cap]
            valid = vmask[:cap]
            x_e = x_flat[idx]
            y_e = _ffn(x_e, W1[e], b1[e], W2[e], b2[e])
            w_tok = (topk_scores * match).sum(-1)
            w = jnp.where(valid, w_tok[idx], 0.0)
            y_flat = y_flat.at[idx].add(y_e * w[:, None])
            y_flat = jnp.where(overflow[:, None], y_fb, y_flat)
            fallback = fallback | overflow
        return y_flat.reshape(B, S, D)

    def _L1_attn_ref(x, decay, Wq, Wv, Wg, Wo, ln_gamma, ln_beta):
        import jax, jax.numpy as jnp
        import numpy as np
        D_MODEL = 128
        NHEAD = 16
        HEAD_DIM = D_MODEL // NHEAD
        B, L = (4, 1024)
        LN_EPS = 1e-05

        def _decay_scan(v, lam):
            a = jnp.broadcast_to(lam[None, None, :, None], v.shape)

            def combine(c1, c2):
                a1, b1 = c1
                a2, b2 = c2
                return (a1 * a2, b1 * a2 + b2)
            _, state = jax.lax.associative_scan(combine, (a, v), axis=1)
            return state

        def _layernorm(y, gamma, beta):
            mu = jnp.mean(y, axis=-1, keepdims=True)
            var = jnp.mean(jnp.square(y - mu), axis=-1, keepdims=True)
            return (y - mu) * jax.lax.rsqrt(var + LN_EPS) * gamma + beta
        Bx, Lx, D = x.shape
        q = (x @ Wq.T).reshape(Bx, Lx, NHEAD, HEAD_DIM)
        v = (x @ Wv.T).reshape(Bx, Lx, NHEAD, HEAD_DIM)
        state = _decay_scan(v, decay)
        y = (q * state).reshape(Bx, Lx, D)
        y = _layernorm(y, ln_gamma, ln_beta)
        gate = jax.nn.silu(x @ Wg.T)
        y = y * gate
        return y @ Wo.T

    def _L1_ffn_ref(x, wqkv, q_scale, k_scale, wo, ln_g, ln_b, w1, b1, w2, b2):
        import jax, jax.numpy as jnp
        import numpy as np
        DIM = 128
        DEPTH = 2
        HEADS = 8
        DIM_HEAD = 64
        WINDOW = 64
        INNER = HEADS * DIM_HEAD
        HID = int(DIM * 4 * 2 / 3)
        B, N = (2, 1024)
        QK_SCALE = 8.0

        def shift_token(t):
            t1, t2 = jnp.split(t, 2, axis=-1)
            t2 = jnp.pad(t2, ((0, 0), (1, 0), (0, 0)))[:, :-1]
            return jnp.concatenate([t1, t2], axis=-1)

        def l2norm(t):
            return t / jnp.clip(jnp.linalg.norm(t, axis=-1, keepdims=True), 1e-12)

        def rotate_half(x):
            x1, x2 = jnp.split(x, 2, axis=-1)
            return jnp.concatenate([-x2, x1], axis=-1)

        def rotary_xpos(q, k):
            n = q.shape[-2]
            half_idx = jnp.arange(0, DIM_HEAD, 2, dtype=jnp.float32)
            inv_freq = 1.0 / 10000.0 ** (half_idx / DIM_HEAD)
            t = jnp.arange(n, dtype=jnp.float32)
            freqs = t[:, None] * inv_freq[None, :]
            freqs = jnp.concatenate([freqs, freqs], axis=-1)
            base = (half_idx + 0.4 * DIM_HEAD) / (1.4 * DIM_HEAD)
            power = (t - n // 2) / float(WINDOW // 2)
            scale = base[None, :] ** power[:, None]
            scale = jnp.concatenate([scale, scale], axis=-1)
            cos, sin = (jnp.cos(freqs), jnp.sin(freqs))
            q = q * cos * scale + rotate_half(q) * sin * scale
            k = k * cos / scale + rotate_half(k) * sin / scale
            return (q, k)

        def local_attention(q, k, v):
            b, h, n, d = q.shape
            w = n // WINDOW
            bq = q.reshape(b, h, w, WINDOW, d) * QK_SCALE
            bk = k.reshape(b, h, w, WINDOW, d)
            bv = v.reshape(b, h, w, WINDOW, d)

            def look_around(t):
                p = jnp.pad(t, ((0, 0), (0, 0), (1, 0), (0, 0), (0, 0)))
                return jnp.concatenate([p[:, :, :w], p[:, :, 1:]], axis=3)
            bk, bv = (look_around(bk), look_around(bv))
            bt = jnp.arange(n).reshape(w, WINDOW)
            btp = jnp.pad(bt, ((1, 0), (0, 0)), constant_values=-1)
            btk = jnp.concatenate([btp[:w], btp[1:]], axis=1)
            sim = jnp.einsum('bhwid,bhwjd->bhwij', bq, bk)
            i = bt[:, :, None]
            j = btk[:, None, :]
            mask = (i < j) | (i > j + WINDOW) | (j == -1)
            sim = jnp.where(mask, -jnp.finfo(sim.dtype).max, sim)
            attn = jax.nn.softmax(sim, axis=-1)
            out = jnp.einsum('bhwij,bhwjd->bhwid', attn, bv)
            return out.reshape(b, h, n, d)

        def _layer(x, wqkv, qs, ksc, wo, lg, lb, w1, b1, w2, b2):
            b, n, _ = x.shape
            h = shift_token(x)
            qkv = h @ wqkv
            q, k, v = jnp.split(qkv, 3, axis=-1)
            to_heads = lambda t: t.reshape(b, n, HEADS, DIM_HEAD).transpose(0, 2, 1, 3)
            q, k, v = (to_heads(q), to_heads(k), to_heads(v))
            q = l2norm(q) * qs
            k = l2norm(k) * ksc
            q, k = rotary_xpos(q, k)
            o = local_attention(q, k, v)
            o = o.transpose(0, 2, 1, 3).reshape(b, n, INNER)
            x = x + o @ wo
            h = shift_token(x)
            mu = h.mean(-1, keepdims=True)
            var = h.var(-1, keepdims=True)
            h = (h - mu) / jnp.sqrt(var + 1e-05) * lg + lb
            h = h @ w1 + b1
            a, g = jnp.split(h, 2, axis=-1)
            h = a * jax.nn.gelu(g, approximate=False)
            x = x + h @ w2 + b2
            return x
        for l in range(DEPTH):
            x = _layer(x, wqkv[l], q_scale[l], k_scale[l], wo[l], ln_g[l], ln_b[l], w1[l], b1[l], w2[l], b2[l])
        return x
    x = L0_attn_x
    x = x + _L0_attn_ref(_layernorm(x, axis=-1), L0_attn_Wq, L0_attn_Wk, L0_attn_Wv, L0_attn_Wbeta, L0_attn_bbeta, L0_attn_Wmix, L0_attn_bmix, L0_attn_Wout, L0_attn_bout, L0_attn_ln_g, L0_attn_ln_b)
    x = x + _L0_ffn_ref(_layernorm(x, axis=-1), L0_ffn_Wr, L0_ffn_W1, L0_ffn_b1, L0_ffn_W2, L0_ffn_b2, L0_ffn_fw1, L0_ffn_fb1, L0_ffn_fw2, L0_ffn_fb2)
    x = x + _L1_attn_ref(_layernorm(x, axis=-1), L1_attn_decay, L1_attn_Wq, L1_attn_Wv, L1_attn_Wg, L1_attn_Wo, L1_attn_ln_gamma, L1_attn_ln_beta)
    x = x + _L1_ffn_ref(_layernorm(x, axis=-1), L1_ffn_wqkv, L1_ffn_q_scale, L1_ffn_k_scale, L1_ffn_wo, L1_ffn_ln_g, L1_ffn_ln_b, L1_ffn_w1, L1_ffn_b1, L1_ffn_w2, L1_ffn_b2)
    return x

_drawn_inputs = setup_inputs


def setup_inputs(seed=0):
    import zlib

    import numpy as np

    out = dict(_drawn_inputs(seed))
    spreads = {'L0_attn_Wmix': (0.0, 0.1),
     'L0_attn_bmix': (0.0, 2.0),
     'L0_attn_bout': (0.0, 0.1),
     'L0_attn_ln_g': (1.0, 0.2),
     'L0_attn_ln_b': (0.0, 0.1),
     'L0_ffn_b1': (0.0, 0.732),
     'L0_ffn_b2': (0.0, 0.1),
     'L0_ffn_fb1': (0.0, 0.1),
     'L0_ffn_fb2': (0.0, 0.1),
     'L1_attn_ln_gamma': (1.0, 0.2),
     'L1_attn_ln_beta': (0.0, 0.281),
     'L1_ffn_q_scale': (1.0, 0.6),
     'L1_ffn_k_scale': (1.0, 0.6),
     'L1_ffn_ln_g': (1.0, 0.6),
     'L1_ffn_ln_b': (0.0, 0.8),
     'L1_ffn_b1': (0.0, 0.8),
     'L1_ffn_b2': (0.0, 0.8)}
    factors = {'L0_attn_Wq': 2.775,
     'L0_attn_Wbeta': 6.839,
     'L0_ffn_W1': 2.743,
     'L1_ffn_wqkv': 4.727,
     'L1_ffn_wo': 4.758,
     'L1_ffn_w1': 8.0,
     'L1_ffn_w2': 8.0}
    for name, (base, spread) in spreads.items():
        noise = np.random.default_rng([zlib.crc32(name.encode()), seed]).standard_normal(out[name].shape)
        drawn = base * np.exp(spread * noise) if base else spread * noise
        out[name] = jnp.asarray(drawn.astype(out[name].dtype))
    for name, factor in factors.items():
        out[name] = (out[name] * factor).astype(out[name].dtype)
    return out
```

```python
from collections import namedtuple
from contextlib import ExitStack

import concourse.bass as bass
from concourse import mybir

F32 = mybir.dt.float32
BF16 = mybir.dt.bfloat16
ALU = mybir.AluOpType
ACT = mybir.ActivationFunctionType
AX = mybir.AxisListType

P = 128
NSEQ, SEQ = 16, 256
T = NSEQ * SEQ
CH = 512
NCH = T // CH
SPC = CH // SEQ
NT = T // P
LN_EPS = 1e-5

NH0, D0, M0 = 32, 4, 2
BMIN, BMAX, DEN_EPS = 0.85, 0.9995, 1e-6
NE = 8
CAP = int(1.25 * (T * 2 / NE))
FFI = 512
NJ = FFI // P
NX = NE + 1
NPART = 3
DEPTH, HEADS, DH, WIN = 2, 8, 64, 64
INNER = HEADS * DH
NB = INNER // P
HID = 341
QK_SCALE = 8.0
LNEXP = "natural_log_exp_and_others"
CLIP2 = 1e-24
LN_SHIFT = 18


def hid_rows(j):
    return min(P, HID - j * P)


NHB = (HID + P - 1) // P


def chunk(c):
    return bass.ds(c * CH, CH)


class Kernel:

    def __init__(self, nc, dram, out, ctx):
        self.nc, self.dram, self.out, self.ctx = nc, dram, out, ctx
        self.started = ctx.enter_context(nc.semaphore("started"))
        self.ps = [ctx.enter_context(nc.psum_tensor(f"bank{i}", [P, CH], F32)) for i in range(8)]

    def sb(self, name, shape, dt=F32, ctx=None):
        return (ctx or self.ctx).enter_context(self.nc.sbuf_tensor(name, shape, dt))


def wait_alone(k, eng, sem, value):
    value = eng.snap(value)
    eng.wait_ge(k.started, 1)
    eng.wait_ge(sem, value)


LnSems = namedtuple("LnSems", "centred squared var logged rstd normed")
LnBuffers = namedtuple("LnBuffers", "sq lg rs x v")


def ln_sems(nc, ctx, name):
    return LnSems(*(ctx.enter_context(nc.semaphore(f"{name}_{n}")) for n in LnSems._fields))


def ln_buffers(k, ctx, name, bank_x, bank_v):
    return LnBuffers(sq=k.sb(f"{name}_sq", [P, CH], ctx=ctx), lg=k.sb(f"{name}_lg", [P, CH], ctx=ctx),
                           rs=k.sb(f"{name}_rs", [P, CH], ctx=ctx), x=k.ps[bank_x], v=k.ps[bank_v])


def ln_centre(k, pe, s, b, n, src):
    pe.wait_ge(s.normed, n)
    k.nc.tensor.matmul(b.x[:], k.const["centre"][:], src, start=True, stop=True).then_inc(s.centred, 1)


def ln_variance(k, pe, s, b, n):
    pe.wait_ge(s.squared, n)
    k.nc.tensor.matmul(b.v[:], k.const["mean"][:], b.sq[:], start=True, stop=True).then_inc(s.var, 1)


def ln_rstd(k, act, s, b, n):
    act.wait_ge(s.centred, n)
    k.nc.scalar.activation(b.sq[:], b.x[:], ACT.Square).then_inc(s.squared, 1)
    act.wait_ge(s.var, n)
    k.nc.scalar.activation(b.lg[:], b.v[:], ACT.Ln, bias=k.eps[:, 0:1]).then_inc(s.logged, 1)
    act.wait_ge(s.logged, n)
    k.nc.scalar.activation(b.rs[:], b.lg[:], ACT.Exp, scale=-0.5).then_inc(s.rstd, 1)


def ln_scale(k, dve, s, b, n, dst):
    dve.wait_ge(s.rstd, n)
    k.nc.vector.tensor_tensor(dst, b.x[:], b.rs[:], ALU.mult).then_inc(s.normed, 1)


def load(k):
    nc = k.nc
    k.XT = k.sb("XT", [P, T])
    k.H = k.sb("H", [P, T])
    k.const = {}
    k.eps = k.sb("eps", [P, 1])
    small = ["ident", "centre", "mean", "identb", "headmean", "mask_q", "mask_k"]
    for n in small:
        v = k.dram[n]
        k.const[n] = k.sb(n, list(v.shape), v.dtype)
    xf = k.dram["x"].rearrange("b t d -> (b t) d").rearrange("(n p) d -> p n d", p=P)
    with ExitStack() as ctx:
        tok = k.sb("tok", [P, NT, P], ctx=ctx)
        sem = lambda n: ctx.enter_context(nc.semaphore(n))
        x_in, const_in, turned, stored = map(sem, ("x_in", "const_in", "x_turned", "x_stored"))
        block = ctx.enter_context(nc.Block())

        @block.sync
        def _(sp):
            for i, n in enumerate(small):
                sp.dma_start(k.const[n][:], k.dram[n]).then_inc(const_in, 16)
            for q in range(NCH):
                sp.dma_start(tok[:, 4 * q:4 * q + 4, :], xf[:, 4 * q:4 * q + 4, :]).then_inc(x_in, 16)

        @block.tensor
        def _(pe):
            pe.wait_ge(const_in, 16 * len(small))
            pe.wait_ge(x_in, 16 * NCH)
            for n in range(NT):
                if n % 4 == 0 and n >= 8:
                    pe.wait_ge(stored, n // 4 - 1)
                t = nc.tensor.transpose(k.ps[(n // 4) % 2][:, (n % 4) * P:(n % 4 + 1) * P], tok[:, n, :], k.const["ident"][:])
                if n % 4 == 3:
                    t.then_inc(turned, 1)

        @block.scalar
        def _(act):
            for q in range(NCH):
                act.wait_ge(turned, q + 1)
                nc.scalar.activation(k.XT[:, q * CH:(q + 1) * CH], k.ps[q % 2][:], ACT.Copy).then_inc(stored, 1)

        @block.vector
        def _(dve):
            nc.vector.memset(k.eps[:], LN_EPS).then_inc(k.started, 1)
            dve.wait_ge(k.started, 1)


def store(k):
    nc = k.nc
    of = k.out.rearrange("b t d -> (b t) d").rearrange("(n p) d -> p n d", p=P)
    with ExitStack() as ctx:
        tok = k.sb("tok_out", [P, NT, P], ctx=ctx)
        sem = lambda n: ctx.enter_context(nc.semaphore(n))
        total, turned, copied, written = map(sem, ("total", "y_turned", "y_copied", "y_written"))
        block = ctx.enter_context(nc.Block())

        @block.vector
        def _(dve):
            for q in range(NCH):
                cols = slice(q * CH, (q + 1) * CH)
                nc.vector.tensor_tensor(k.XT[:, cols], k.XT[:, cols], k.H[:, cols], ALU.add).then_inc(total, 1)

        @block.tensor
        def _(pe):
            for n in range(NT):
                pe.wait_ge(total, n // 4 + 1)
                if n % 4 == 0 and n >= 8:
                    pe.wait_ge(copied, n // 4 - 1)
                t = nc.tensor.transpose(k.ps[(n // 4) % 2][:, (n % 4) * P:(n % 4 + 1) * P],
                                        k.XT[:, n * P:(n + 1) * P], k.const["ident"][:])
                if n % 4 == 3:
                    t.then_inc(turned, 1)

        @block.scalar
        def _(act):
            for q in range(NCH):
                act.wait_ge(turned, q + 1)
                nc.scalar.activation(tok[:, 4 * q:4 * q + 4, :], k.ps[q % 2][:].rearrange("p (a b) -> p a b", a=4),
                                     ACT.Copy).then_inc(copied, 1)

        @block.sync
        def _(sp):
            for q in range(NCH):
                sp.wait_ge(copied, q + 1)
                sp.dma_start(of[:, 4 * q:4 * q + 4, :], tok[:, 4 * q:4 * q + 4, :]).then_inc(written, 16)
            sp.wait_ge(written, 16 * NCH)


def norm_stage(k, name):
    nc = k.nc
    with ExitStack() as ctx:
        b = ln_buffers(k, ctx, name, 0, 1)
        s = ln_sems(nc, ctx, name)
        block = ctx.enter_context(nc.Block())

        @block.tensor
        def _(pe):
            with pe.Fori(0, NCH) as c:
                ln_centre(k, pe, s, b, c + 1, k.XT[:, chunk(c)])
                ln_variance(k, pe, s, b, c + 1)

        @block.scalar
        def _(act):
            nc.scalar.preload_act_table_set(LNEXP)
            with act.Fori(0, NCH) as c:
                ln_rstd(k, act, s, b, c + 1)

        @block.vector
        def _(dve):
            dve.sem_inc(s.normed, 1)
            with dve.Fori(0, NCH) as c:
                ln_scale(k, dve, s, b, c + 1, k.H[:, chunk(c)])


def linear_attention(k):
    nc, ps = k.nc, k.ps
    with ExitStack() as big:
        names = ["wq0", "wq0s", "wk0", "wk0s", "wv0", "wbeta", "wmix", "wout0", "vec0", "rope0", "spread", "headsum"]
        w = {}
        for n in names:
            w[n] = k.sb(n, list(k.dram[n].shape), F32, big)
        beta = [k.sb(f"beta{m}", [P, T], ctx=big) for m in range(M0)]
        mix = [k.sb(f"mix{m}", [P, T], ctx=big) for m in range(M0)]
        Y = k.sb("Y0", [P, T], ctx=big)
        wmixd = k.sb("wmixd", [P, P], ctx=big)
        bd = k.sb("bmixd", [P, 2], ctx=big)
        with ExitStack() as ctx:
            sem = lambda n: ctx.enter_context(nc.semaphore(n))
            w_in, diff, logits, gates, clipped = map(sem, ("w0_in", "mix_diff", "gate_logits", "gate_values", "beta_clipped"))
            block = ctx.enter_context(nc.Block())

            @block.sync
            def _(sp):
                for n in names:
                    sp.dma_start(w[n][:], k.dram[n]).then_inc(w_in, 16)

            @block.tensor
            def _(pe):
                pe.wait_ge(w_in, 16 * len(names))
                pe.wait_ge(diff, 3)
                with pe.Fori(0, NCH) as c:
                    pe.wait_ge(gates, c * 4 + 4)
                    for m in range(M0):
                        nc.tensor.matmul(ps[m][:], w["wbeta"][:, m, :], k.H[:, chunk(c)], start=True, stop=True)
                    nc.tensor.matmul(ps[2][:], wmixd[:], k.H[:, chunk(c)], start=True, stop=True).then_inc(logits, 1)

            @block.scalar
            def _(act):
                act.sem_inc(gates, 4)
                act.wait_ge(w_in, 16 * len(names))
                act.wait_ge(diff, 3)
                with act.Fori(0, NCH) as c:
                    act.wait_ge(logits, c + 1)
                    for m in range(M0):
                        nc.scalar.activation(beta[m][:, chunk(c)], ps[m][:], ACT.Sigmoid,
                                             bias=w["vec0"][:, m:m + 1]).then_inc(gates, 1)
                    nc.scalar.activation(mix[0][:, chunk(c)], ps[2][:], ACT.Sigmoid, bias=bd[:, 0:1]).then_inc(gates, 1)
                    nc.scalar.activation(mix[1][:, chunk(c)], ps[2][:], ACT.Sigmoid, bias=bd[:, 1:2],
                                         scale=-1.0).then_inc(gates, 1)

            @block.vector
            def _(dve):
                dve.wait_ge(w_in, 16 * len(names))
                nc.vector.tensor_tensor(wmixd[:], w["wmix"][:, 0, :], w["wmix"][:, 1, :], ALU.subtract).then_inc(diff, 1)
                nc.vector.tensor_tensor(bd[:, 0:1], w["vec0"][:, 2:3], w["vec0"][:, 3:4], ALU.subtract).then_inc(diff, 1)
                nc.vector.tensor_tensor(bd[:, 1:2], w["vec0"][:, 3:4], w["vec0"][:, 2:3], ALU.subtract).then_inc(diff, 1)
                with dve.Fori(0, NCH) as c:
                    dve.wait_ge(gates, c * 4 + 8)
                    for m in range(M0):
                        nc.vector.tensor_scalar(beta[m][:, chunk(c)], beta[m][:, chunk(c)], BMIN, BMAX,
                                                ALU.max, ALU.min).then_inc(clipped, 1)
                dve.wait_ge(clipped, 2 * NCH)
                for m in range(M0):
                    nc.vector.memset(beta[m][:].rearrange("p (s t) -> p s t", t=SEQ)[:, :, 0:1], 0.0)

        with ExitStack() as ctx:
            buf = lambda n: k.sb(n, [P, CH], ctx=ctx)
            qa, qb_, ka, kb_, q1, k1, eq, ek = map(buf, ("qa", "qb_", "ka", "kb_", "q1", "k1", "eq", "ek"))
            phq, phk, vs = map(buf, ("phq", "phk", "vs"))
            U = [buf(f"U{d}") for d in range(D0)]
            S = [buf(f"S{i}") for i in range(2)]
            K = [buf(f"K{m}") for m in range(M0)]
            TT = [[buf(f"T{m}_{d}") for d in range(D0)] for m in range(M0)]
            lden = [buf(f"lden{m}") for m in range(M0)]
            deps = k.sb("deps", [P, 1], ctx=ctx)
            sem = lambda n: ctx.enter_context(nc.semaphore(n))
            (q_mm, k_mm, v_mm, rot, rope_sum, plus1, exped, phi, v_sb, pk_mm, u_done, pq_mm, k_scan, s_scan, t_done,
             kp_done, den_mm, ln_den, rden, coef, sum1, sum2, weighted, y_done, eps_set) = map(sem, (
                 "q_mm", "k_mm", "v_mm", "rot", "rope_sum", "plus1", "exped", "phi", "v_sb", "pk_mm", "u_done", "pq_mm",
                 "k_scan", "s_scan", "t_done", "kp_done", "den_mm", "ln_den", "rden", "coef", "sum1", "sum2", "weighted",
                 "y_done", "deps_set"))
            block = ctx.enter_context(nc.Block())

            @block.tensor
            def _(pe):
                with pe.Fori(0, NCH) as c:
                    h = k.H[:, chunk(c)]
                    pe.wait_ge(ln_den, 2 * c + 2)
                    nc.tensor.matmul(ps[0][:], w["wq0"][:], h, start=True, stop=True)
                    nc.tensor.matmul(ps[1][:], w["wq0s"][:], h, start=True, stop=True).then_inc(q_mm, 1)
                    pe.wait_ge(u_done, 4 * c + 4)
                    nc.tensor.matmul(ps[2][:], w["wk0"][:], h, start=True, stop=True)
                    nc.tensor.matmul(ps[3][:], w["wk0s"][:], h, start=True, stop=True).then_inc(k_mm, 1)
                    pe.wait_ge(t_done, 8 * c + 8)
                    nc.tensor.matmul(ps[4][:], w["wv0"][:], h, start=True, stop=True).then_inc(v_mm, 1)
                    pe.wait_ge(phi, 2 * c + 2)
                    for d in range(D0):
                        nc.tensor.matmul(ps[d][:], w["spread"][:, d, :], phk[:], start=True, stop=True).then_inc(pk_mm, 1)
                    pe.wait_ge(v_sb, c + 1)
                    for d in range(D0):
                        nc.tensor.matmul(ps[4 + d][:], w["spread"][:, d, :], phq[:], start=True, stop=True).then_inc(pq_mm, 1)
                    for m in range(M0):
                        pe.wait_ge(kp_done, 2 * c + m + 1)
                        pe.wait_ge(u_done, 4 * c + m + 5)
                        nc.tensor.matmul(ps[m][:], w["headsum"][:], K[m][:], start=True, stop=True).then_inc(den_mm, 1)

            @block.scalar
            def _(act):
                act.sem_inc(ln_den, 2)
                nc.scalar.preload_act_table_set(LNEXP)
                act.wait_ge(eps_set, 1)
                with act.Fori(0, NCH) as c:
                    act.wait_ge(v_mm, c + 1)
                    act.wait_ge(u_done, 4 * c + 4)
                    nc.scalar.activation(vs[:], ps[4][:], ACT.Copy).then_inc(v_sb, 1)
                    act.wait_ge(rope_sum, 2 * c + 1)
                    nc.scalar.activation(ek[:], ka[:], ACT.Exp).then_inc(exped, 1)
                    act.wait_ge(rope_sum, 2 * c + 2)
                    nc.scalar.activation(eq[:], qa[:], ACT.Exp).then_inc(exped, 1)
                    act.wait_ge(y_done, c + 1)
                    for m in range(M0):
                        act.wait_ge(den_mm, 2 * c + m + 1)
                        nc.scalar.activation(lden[m][:], ps[m][:], ACT.Ln, bias=deps[:, 0:1]).then_inc(ln_den, 1)
                        act.wait_ge(ln_den, 2 * c + m + 3)
                        nc.scalar.activation(lden[m][:], lden[m][:], ACT.Exp, scale=-1.0).then_inc(rden, 1)

            @block.vector
            def _(dve):
                nc.vector.memset(deps[:], DEN_EPS).then_inc(eps_set, 1)
                dve.sem_inc(t_done, 8)
                dve.sem_inc(u_done, 4)
                cos, sin = w["rope0"][:, 0, :], w["rope0"][:, 1, :]
                with dve.Fori(0, NCH) as c:
                    dve.wait_ge(k_mm, c + 1)
                    nc.vector.tensor_tensor(ka[:], ps[2][:], cos, ALU.mult)
                    nc.vector.tensor_tensor(kb_[:], ps[3][:], sin, ALU.mult).then_inc(rot, 1)
                    dve.wait_ge(q_mm, c + 1)
                    nc.vector.tensor_tensor(qa[:], ps[0][:], cos, ALU.mult)
                    nc.vector.tensor_tensor(qb_[:], ps[1][:], sin, ALU.mult).then_inc(rot, 1)
                    dve.wait_ge(exped, 2 * c + 1)
                    dve.wait_ge(plus1, 2 * c + 1)
                    nc.vector.scalar_tensor_tensor(phk[:], ek[:], 1.0, k1[:], ALU.min, ALU.max).then_inc(phi, 1)
                    dve.wait_ge(exped, 2 * c + 2)
                    dve.wait_ge(plus1, 2 * c + 2)
                    nc.vector.scalar_tensor_tensor(phq[:], eq[:], 1.0, q1[:], ALU.min, ALU.max).then_inc(phi, 1)
                    dve.wait_ge(phi, 2 * c + 1)
                    for m in range(M0):
                        nc.vector.tensor_tensor_scan(K[m][:], beta[m][:, chunk(c)], phk[:], 0.0,
                                                     ALU.mult, ALU.add).then_inc(k_scan, 1)
                    dve.wait_ge(v_sb, c + 1)
                    for d in range(D0):
                        dve.wait_ge(pk_mm, 4 * c + d + 1)
                        nc.vector.tensor_tensor(U[d][:], ps[d][:], vs[:], ALU.mult).then_inc(u_done, 1)
                    dve.wait_ge(y_done, c + 1)
                    for i in range(2 * D0 + 1):
                        if i < 2 * D0:
                            d, m = i // 2, i % 2
                            if m == 0:
                                dve.wait_ge(u_done, 4 * c + d + 5)
                            dve.wait_ge(t_done, 8 * c + i + 7)
                            nc.vector.tensor_tensor_scan(S[i % 2][:], beta[m][:, chunk(c)], U[d][:], 0.0,
                                                         ALU.mult, ALU.add).then_inc(s_scan, 1)
                        if i > 0:
                            d, m = (i - 1) // 2, (i - 1) % 2
                            if m == 0:
                                dve.wait_ge(pq_mm, 4 * c + d + 1)
                            dve.wait_ge(s_scan, 8 * c + i)
                            nc.vector.tensor_tensor(TT[m][d][:], ps[4 + d][:], S[(i - 1) % 2][:],
                                                    ALU.mult).then_inc(t_done, 1)
                    dve.wait_ge(den_mm, 2 * c + 2)

            @block.gpsimd
            def _(pool):
                pool.sem_inc(y_done, 1)
                with pool.Fori(0, NCH) as c:
                    for i, (a, b, o) in enumerate(((ka, kb_, k1), (qa, qb_, q1))):
                        wait_alone(k, pool, rot, 2 * c + i + 1)
                        nc.gpsimd.tensor_tensor(a[:], a[:], b[:], ALU.add).then_inc(rope_sum, 1)
                        wait_alone(k, pool, rope_sum, 2 * c + i + 1)
                        nc.gpsimd.tensor_scalar(o[:], a[:], 1.0, None, ALU.add).then_inc(plus1, 1)
                    wait_alone(k, pool, phi, 2 * c + 2)
                    for m in range(M0):
                        wait_alone(k, pool, k_scan, 2 * c + m + 1)
                        nc.gpsimd.tensor_tensor(K[m][:], K[m][:], phq[:], ALU.mult).then_inc(kp_done, 1)
                    for m in range(M0):
                        wait_alone(k, pool, rden, 2 * c + m + 1)
                        nc.gpsimd.tensor_tensor(lden[m][:], lden[m][:], mix[m][:, chunk(c)], ALU.mult).then_inc(coef, 1)
                    for m in range(M0):
                        for d in (0, 2):
                            wait_alone(k, pool, t_done, 8 * c + 2 * (d + 1) + m + 9)
                            nc.gpsimd.tensor_tensor(TT[m][d][:], TT[m][d][:], TT[m][d + 1][:],
                                                    ALU.add).then_inc(sum1, 1)
                        wait_alone(k, pool, sum1, 4 * c + 2 * m + 2)
                        nc.gpsimd.tensor_tensor(TT[m][0][:], TT[m][0][:], TT[m][2][:], ALU.add).then_inc(sum2, 1)
                        wait_alone(k, pool, sum2, 2 * c + m + 1)
                        wait_alone(k, pool, coef, 2 * c + m + 1)
                        nc.gpsimd.tensor_tensor(TT[m][0][:], TT[m][0][:], lden[m][:], ALU.mult).then_inc(weighted, 1)
                    wait_alone(k, pool, weighted, 2 * c + 2)
                    nc.gpsimd.tensor_tensor(Y[:, chunk(c)], TT[0][0][:], TT[1][0][:], ALU.add).then_inc(y_done, 1)

        with ExitStack() as ctx:
            z = k.sb("z", [P, CH], ctx=ctx)
            zn = k.sb("zn", [P, CH], ctx=ctx)
            b1, b2 = ln_buffers(k, ctx, "nz", 1, 2), ln_buffers(k, ctx, "nx", 3, 4)
            s1, s2 = ln_sems(nc, ctx, "nz"), ln_sems(nc, ctx, "nx")
            sem = lambda n: ctx.enter_context(nc.semaphore(n))
            o_mm, z_done, affine, resid = map(sem, ("o_mm", "z_done", "affine0", "resid0"))
            block = ctx.enter_context(nc.Block())

            @block.tensor
            def _(pe):
                with pe.Fori(0, NCH) as c:
                    pe.wait_ge(z_done, c + 1)
                    nc.tensor.matmul(ps[0][:], w["wout0"][:], Y[:, chunk(c)], start=True, stop=True).then_inc(o_mm, 1)
                    pe.wait_ge(z_done, c + 2)
                    ln_centre(k, pe, s1, b1, c + 1, z[:])
                    ln_variance(k, pe, s1, b1, c + 1)
                    pe.wait_ge(resid, c + 1)
                    ln_centre(k, pe, s2, b2, c + 1, k.XT[:, chunk(c)])
                    ln_variance(k, pe, s2, b2, c + 1)

            @block.scalar
            def _(act):
                nc.scalar.preload_act_table_set(LNEXP)
                with act.Fori(0, NCH) as c:
                    ln_rstd(k, act, s1, b1, c + 1)
                    ln_rstd(k, act, s2, b2, c + 1)

            @block.vector
            def _(dve):
                dve.sem_inc(s1.normed, 1)
                dve.sem_inc(s2.normed, 1)
                dve.sem_inc(z_done, 1)
                with dve.Fori(0, NCH) as c:
                    dve.wait_ge(o_mm, c + 1)
                    nc.vector.scalar_tensor_tensor(z[:], ps[0][:], w["vec0"][:, 4:5], k.H[:, chunk(c)],
                                                   ALU.add, ALU.add).then_inc(z_done, 1)
                    ln_scale(k, dve, s1, b1, c + 1, zn[:])
                    dve.wait_ge(s1.normed, c + 2)
                    nc.vector.tensor_scalar(zn[:], zn[:], w["vec0"][:, 5:6], w["vec0"][:, 6:7],
                                            ALU.mult, ALU.add).then_inc(affine, 1)
                    dve.wait_ge(affine, c + 1)
                    nc.vector.tensor_tensor(k.XT[:, chunk(c)], k.XT[:, chunk(c)], zn[:], ALU.add).then_inc(resid, 1)
                    ln_scale(k, dve, s2, b2, c + 1, k.H[:, chunk(c)])


def experts(k):
    nc, ps = k.nc, k.ps
    with ExitStack() as big:
        names = ["wr", "iota8", "tri", "ones", "w1e", "w2e", "b1e", "b2e", "pick"]
        w = {}
        for n in names:
            w[n] = k.sb(n, list(k.dram[n].shape), k.dram[n].dtype, big)
        wT = k.sb("wT", [P, T], BF16, big)
        with ExitStack() as ctx:
            s3 = lambda n, e=NE, d=F32: k.sb(n, [P, NT, e], d, ctx)
            pr, oh1, oh2, val, eq, Wt = (s3(n) for n in ("probs", "oh1", "oh2", "val", "eqm", "Wt"))
            W9, R9 = s3("W9", NX), s3("R9", NX)
            parts = s3("parts", NPART * NX, BF16)
            cols = k.sb("cols", [P, 14, NT], F32, ctx)
            mx, sm, rs_, p1, v1, p2, v2, w1, w2, fb, pos, inc, over, one = (cols[:, i, :] for i in range(14))
            elig = k.sb("elig", [P, NT], BF16, ctx)
            eligf = k.sb("eligf", [P, NT], F32, ctx)
            sem = lambda n: ctx.enter_context(nc.semaphore(n))
            w_in, r_in, wT_zero, logit_mm, shifted, exped, step, elig_r, counted, parts_r, turned, turned_sb = map(sem, (
                "we_in", "wr_in", "wT_zero", "logit_mm", "shifted", "exped_r", "dve_step", "elig_r", "counted", "parts_r", "turned",
                "turned_sb"))
            block = ctx.enter_context(nc.Block())
            bc = lambda a: a.rearrange("p (n o) -> p n o", o=1).to_broadcast([P, NT, NE])

            @block.sync
            def _(sp):
                for n in names[:4]:
                    sp.dma_start(w[n][:], k.dram[n]).then_inc(r_in, 16)
                for n in names[4:]:
                    sp.dma_start(w[n][:], k.dram[n]).then_inc(w_in, 16)
                sp.wait_ge(w_in, 16 * 5)

            @block.tensor
            def _(pe):
                pe.wait_ge(r_in, 64)
                for n in range(NT):
                    i = nc.tensor.matmul(ps[0][:, n * NE:(n + 1) * NE], k.H[:, n * P:(n + 1) * P], w["wr"][:],
                                         start=True, stop=True)
                i.then_inc(logit_mm, 1)
                for e in range(NE):
                    pe.wait_ge(elig_r, e + 1)
                    nc.tensor.matmul(ps[1][:, 0:NT], w["tri"][:], elig[:], start=True, stop=True)
                    nc.tensor.matmul(ps[2][:, 0:NT], w["ones"][:], elig[:], start=True, stop=True).then_inc(counted, 1)
                pe.wait_ge(parts_r, 1)
                for n in range(NT):
                    bank = ps[3 + n // 8][:].bitcast(BF16)
                    i = nc.tensor.transpose(bank[0:NPART * NX, (n % 8) * P:(n % 8 + 1) * P], parts[:, n, :], k.const["identb"][:])
                    if n % 8 == 7:
                        i.then_inc(turned, 1)

            @block.gpsimd
            def _(pool):
                nc.gpsimd.memset(wT[:], 0.0).then_inc(wT_zero, 1)

            @block.scalar
            def _(act):
                act.wait_ge(shifted, 1)
                nc.scalar.activation(pr[:], pr[:], ACT.Exp).then_inc(exped, 1)
                act.wait_ge(wT_zero, 1)
                for q in range(NT // 8):
                    act.wait_ge(turned, q + 1)
                    nc.scalar.activation(wT[0:NPART * NX, q * 8 * P:(q + 1) * 8 * P], ps[3 + q][:].bitcast(BF16)[0:NPART * NX, :],
                                         ACT.Copy).then_inc(turned_sb, 1)
                act.wait_ge(turned_sb, NT // 8)

            @block.vector
            def _(dve):
                V = nc.vector
                done = [0]

                def after(ins):
                    done[0] += 1
                    ins.then_inc(step, 1)
                    dve.wait_ge(step, done[0])

                dve.wait_ge(r_in, 64)
                dve.wait_ge(logit_mm, 1)
                lg = ps[0][:, 0:NT * NE].rearrange("p (n e) -> p n e", e=NE)
                after(V.tensor_reduce(mx, lg, AX.X, ALU.max))
                V.tensor_tensor(pr[:], lg, bc(mx), ALU.subtract).then_inc(shifted, 1)
                dve.wait_ge(exped, 1)
                after(V.tensor_reduce(sm, pr[:], AX.X, ALU.add))
                after(V.reciprocal(rs_, sm))
                after(V.tensor_tensor(pr[:], pr[:], bc(rs_), ALU.mult))
                for p_, v_, oh in ((p1, v1, oh1), (p2, v2, oh2)):
                    after(V.tensor_reduce(p_, pr[:], AX.X, ALU.max))
                    after(V.tensor_tensor(eq[:], pr[:], bc(p_), ALU.is_equal))
                    after(V.tensor_tensor(val[:], eq[:], w["iota8"][:], ALU.mult))
                    after(V.tensor_reduce(v_, val[:], AX.X, ALU.min))
                    after(V.tensor_tensor(oh[:], w["iota8"][:], bc(v_), ALU.is_equal))
                    if oh is oh1:
                        after(V.scalar_tensor_tensor(pr[:], oh1[:], -2.0, pr[:], ALU.mult, ALU.add))
                after(V.tensor_tensor(sm, p1, p2, ALU.add))
                after(V.tensor_scalar(sm, sm, 1e-9, None, ALU.max))
                after(V.reciprocal(rs_, sm))
                after(V.tensor_tensor(w1, p1, rs_, ALU.mult))
                after(V.tensor_tensor(w2, p2, rs_, ALU.mult))
                after(V.tensor_tensor(Wt[:], oh1[:], bc(w1), ALU.mult))
                after(V.tensor_tensor(val[:], oh2[:], bc(w2), ALU.mult))
                after(V.tensor_tensor(Wt[:], Wt[:], val[:], ALU.add))
                after(V.tensor_tensor(oh1[:], oh1[:], oh2[:], ALU.add))
                after(V.memset(fb, 0.0))
                after(V.memset(one, 1.0))
                for e in range(NE):
                    after(V.tensor_tensor(eligf[:], oh1[:, :, e], fb, ALU.is_gt))
                    V.tensor_copy(elig[:], eligf[:]).then_inc(elig_r, 1)
                    dve.wait_ge(counted, e + 1)
                    after(V.tensor_tensor_scan(inc, one, ps[2][:, 0:NT], 0.0, ALU.mult, ALU.add))
                    after(V.tensor_tensor(inc, inc, ps[2][:, 0:NT], ALU.subtract))
                    after(V.tensor_tensor(pos, inc, ps[1][:, 0:NT], ALU.add))
                    after(V.scalar_tensor_tensor(over, pos, float(CAP), eligf[:], ALU.is_gt, ALU.mult))
                    after(V.tensor_tensor(fb, fb, over, ALU.max))
                after(V.tensor_tensor(over, one, fb, ALU.subtract))
                after(V.tensor_tensor(W9[:, :, 0:NE], Wt[:], bc(over), ALU.mult))
                after(V.tensor_copy(W9[:, :, NE], fb))
                after(V.tensor_copy(parts[:, :, 0:NX], W9[:]))
                after(V.tensor_tensor(R9[:], W9[:], parts[:, :, 0:NX], ALU.subtract))
                after(V.tensor_copy(parts[:, :, NX:2 * NX], R9[:]))
                after(V.tensor_tensor(R9[:], R9[:], parts[:, :, NX:2 * NX], ALU.subtract))
                after(V.tensor_copy(parts[:, :, 2 * NX:3 * NX], R9[:]))
                dve.sem_inc(parts_r, 1)

        with ExitStack() as ctx:
            G = k.sb("G", [P, 3, NJ, CH], ctx=ctx)
            WE = k.sb("WE", [P, 3, CH], ctx=ctx)
            Z = k.sb("Z", [P, 3, CH], ctx=ctx)
            acc = k.sb("acc", [P, CH], ctx=ctx)
            sem = lambda n: ctx.enter_context(nc.semaphore(n))
            h_mm, gelu, y_mm, spread_mm, spread_sb, z_done, added, resid = map(sem, (
                "h_mm", "gelu", "ye_mm", "spread_mm", "spread_sb", "ze_done", "added", "resid_e"))
            block = ctx.enter_context(nc.Block())

            @block.tensor
            def _(pe):
                pe.sem_inc(y_mm, 3)
                with pe.Fori(0, NCH) as c:
                    for i in range(NX + 1):
                        if i < NX:
                            for j in range(NJ):
                                pe.wait_ge(gelu, (c * NX + i) * NJ + j + 1)
                                nc.tensor.matmul(ps[j][:], w["w1e"][:, i, j * P:(j + 1) * P], k.H[:, chunk(c)],
                                                 start=True, stop=True).then_inc(h_mm, 1)
                        if i > 0:
                            e = i - 1
                            wait_alone(k, pe, spread_sb, c * NX + e + 1)
                            nc.tensor.matmul(ps[7][:], w["pick"][:, e * P:(e + 1) * P], wT[:, chunk(c)],
                                             start=True, stop=True).then_inc(spread_mm, 1)
                            pe.wait_ge(z_done, c * NX + e + 1)
                            pe.wait_ge(gelu, (c * NX + e) * NJ + 2 * NJ)
                            for j in range(NJ):
                                o = nc.tensor.matmul(ps[4 + e % 3][:], w["w2e"][:, e, j, :], G[:, e % 3, j, :],
                                                     start=(j == 0), stop=(j == NJ - 1))
                            o.then_inc(y_mm, 1)

            @block.scalar
            def _(act):
                act.sem_inc(gelu, NJ)
                act.sem_inc(spread_sb, 1)
                nc.scalar.preload_act_table(ACT.Gelu)
                with act.Fori(0, NCH) as c:
                    for i in range(NX + 1):
                        if i < NX:
                            act.wait_ge(y_mm, c * NX + i + 1)
                            for j in range(NJ):
                                act.wait_ge(h_mm, (c * NX + i) * NJ + j + 1)
                                nc.scalar.activation(G[:, i % 3, j, :], ps[j][:], ACT.Gelu,
                                                     bias=w["b1e"][:, i, j:j + 1]).then_inc(gelu, 1)
                        if i > 0:
                            e = i - 1
                            act.wait_ge(spread_mm, c * NX + e + 1)
                            act.wait_ge(z_done, c * NX + e + 1)
                            nc.scalar.activation(WE[:, e % 3, :], ps[7][:], ACT.Copy).then_inc(spread_sb, 1)

            @block.vector
            def _(dve):
                dve.sem_inc(z_done, 3)
                dve.sem_inc(resid, 1)
                with dve.Fori(0, NCH) as c:
                    for e in range(NX):
                        dve.wait_ge(y_mm, c * NX + e + 4)
                        dve.wait_ge(spread_sb, c * NX + e + 2)
                        dve.wait_ge(added, c * NX + e + 1)
                        nc.vector.scalar_tensor_tensor(Z[:, e % 3, :], ps[4 + e % 3][:], w["b2e"][:, e:e + 1],
                                                       WE[:, e % 3, :], ALU.add, ALU.mult).then_inc(z_done, 1)
                    dve.wait_ge(added, (c + 1) * NX + 3)
                    nc.vector.tensor_tensor(k.XT[:, chunk(c)], k.XT[:, chunk(c)], acc[:], ALU.add).then_inc(resid, 1)

            @block.gpsimd
            def _(pool):
                pool.sem_inc(added, 3)
                with pool.Fori(0, NCH) as c:
                    for e in range(1, NX):
                        wait_alone(k, pool, z_done, c * NX + e + 4)
                        if e == 1:
                            wait_alone(k, pool, resid, c + 1)
                            nc.gpsimd.tensor_tensor(acc[:], Z[:, 0, :], Z[:, 1, :], ALU.add).then_inc(added, 2)
                        else:
                            wait_alone(k, pool, added, c * NX + e + 3)
                            nc.gpsimd.tensor_tensor(acc[:], acc[:], Z[:, e % 3, :], ALU.add).then_inc(added, 1)


def retention(k):
    nc, ps = k.nc, k.ps
    with ExitStack() as big:
        names = ["wq1", "wv1", "wg1", "wo1", "vec1"]
        w = {}
        for n in names:
            w[n] = k.sb(n, list(k.dram[n].shape), F32, big)
        G = k.sb("G1", [P, T], ctx=big)
        Y = k.sb("Y1", [P, T], ctx=big)
        with ExitStack() as ctx:
            dec = k.sb("dec", [P, CH], ctx=ctx)
            h = k.sb("h1", [P, CH], ctx=ctx)
            st = k.sb("st1", [P, CH], ctx=ctx)
            y = k.sb("y1", [P, CH], ctx=ctx)
            yn = k.sb("yn1", [P, CH], ctx=ctx)
            b1, b2 = ln_buffers(k, ctx, "na", 0, 1), ln_buffers(k, ctx, "nb", 2, 3)
            s1, s2 = ln_sems(nc, ctx, "na"), ln_sems(nc, ctx, "nb")
            sem = lambda n: ctx.enter_context(nc.semaphore(n))
            w_in, dec_r, v_mm, q_mm, g_mm, g_sb, state, y_r, aff = map(sem, (
                "w1_in", "dec_r", "v1_mm", "q1_mm", "g1_mm", "g1_sb", "state1", "y1_r", "affine1"))
            block = ctx.enter_context(nc.Block())

            @block.sync
            def _(sp):
                for n in names:
                    sp.dma_start(w[n][:], k.dram[n]).then_inc(w_in, 16)

            @block.tensor
            def _(pe):
                pe.wait_ge(w_in, 16 * len(names))
                with pe.Fori(0, NCH) as c:
                    ln_centre(k, pe, s1, b1, c + 1, k.XT[:, chunk(c)])
                    ln_variance(k, pe, s1, b1, c + 1)
                    pe.wait_ge(s1.normed, c + 2)
                    pe.wait_ge(y_r, c + 1)
                    nc.tensor.matmul(ps[4][:], w["wv1"][:], h[:], start=True, stop=True).then_inc(v_mm, 1)
                    nc.tensor.matmul(ps[5][:], w["wq1"][:], h[:], start=True, stop=True).then_inc(q_mm, 1)
                    pe.wait_ge(g_sb, c + 1)
                    nc.tensor.matmul(ps[6][:], w["wg1"][:], h[:], start=True, stop=True).then_inc(g_mm, 1)
                    pe.wait_ge(y_r, c + 2)
                    ln_centre(k, pe, s2, b2, c + 1, y[:])
                    ln_variance(k, pe, s2, b2, c + 1)

            @block.scalar
            def _(act):
                act.sem_inc(g_sb, 1)
                nc.scalar.preload_act_table_set(LNEXP)
                with act.Fori(0, NCH) as c:
                    ln_rstd(k, act, s1, b1, c + 1)
                    act.wait_ge(g_mm, c + 1)
                    nc.scalar.activation(G[:, chunk(c)], ps[6][:], ACT.Copy).then_inc(g_sb, 1)
                    ln_rstd(k, act, s2, b2, c + 1)

            @block.vector
            def _(dve):
                dve.sem_inc(s1.normed, 1)
                dve.sem_inc(s2.normed, 1)
                dve.sem_inc(y_r, 1)
                dve.wait_ge(w_in, 16 * len(names))
                nc.vector.tensor_copy(dec[:], w["vec1"][:, 0:1].to_broadcast([P, CH])).then_inc(dec_r, 1)
                dve.wait_ge(dec_r, 1)
                nc.vector.memset(dec[:].rearrange("p (s t) -> p s t", t=SEQ)[:, :, 0:1], 0.0).then_inc(dec_r, 1)
                dve.wait_ge(dec_r, 2)
                with dve.Fori(0, NCH) as c:
                    ln_scale(k, dve, s1, b1, c + 1, h[:])
                    dve.wait_ge(v_mm, c + 1)
                    nc.vector.tensor_tensor_scan(st[:], dec[:], ps[4][:], 0.0, ALU.mult, ALU.add).then_inc(state, 1)
                    dve.wait_ge(q_mm, c + 1)
                    dve.wait_ge(state, c + 1)
                    nc.vector.tensor_tensor(y[:], ps[5][:], st[:], ALU.mult).then_inc(y_r, 1)
                    ln_scale(k, dve, s2, b2, c + 1, yn[:])
                    dve.wait_ge(s2.normed, c + 2)
                    nc.vector.tensor_scalar(Y[:, chunk(c)], yn[:], w["vec1"][:, 1:2], w["vec1"][:, 2:3],
                                            ALU.mult, ALU.add).then_inc(aff, 1)
                    dve.wait_ge(g_mm, c + 1)
                    dve.wait_ge(aff, c + 1)

        with ExitStack() as ctx:
            sg = k.sb("sg", [P, 2, CH], ctx=ctx)
            sem = lambda n: ctx.enter_context(nc.semaphore(n))
            silu, gated, o_mm, resid = map(sem, ("silu", "gated", "o1_mm", "resid1"))
            block = ctx.enter_context(nc.Block())

            @block.scalar
            def _(act):
                with act.Fori(0, NCH) as c:
                    nc.scalar.activation(G[:, chunk(c)], G[:, chunk(c)], ACT.Silu).then_inc(silu, 1)

            @block.gpsimd
            def _(pool):
                with pool.Fori(0, NCH) as c:
                    wait_alone(k, pool, silu, c + 1)
                    nc.gpsimd.tensor_tensor(Y[:, chunk(c)], Y[:, chunk(c)], G[:, chunk(c)], ALU.mult).then_inc(gated, 1)

            @block.tensor
            def _(pe):
                with pe.Fori(0, NCH // 2) as c2:
                    for i in range(2):
                        pe.wait_ge(gated, 2 * c2 + i + 1)
                        pe.wait_ge(resid, 2 * c2 + i + 1)
                        nc.tensor.matmul(ps[i][:], w["wo1"][:], Y[:, chunk(2 * c2 + i)], start=True, stop=True).then_inc(o_mm, 1)

            @block.vector
            def _(dve):
                dve.sem_inc(resid, 2)
                with dve.Fori(0, NCH // 2) as c2:
                    for i in range(2):
                        dve.wait_ge(o_mm, 2 * c2 + i + 1)
                        cc = chunk(2 * c2 + i)
                        nc.vector.tensor_tensor(k.XT[:, cc], ps[i][:], k.XT[:, cc], ALU.add).then_inc(resid, 1)


def shift_tokens(k, done, dst, cols):
    nc = k.nc
    nc.vector.tensor_copy(dst[0:64, :], k.H[0:64, cols])
    late = dst[64:P, :].rearrange("p (s t) -> p s t", t=SEQ)[:, :, 1:SEQ]
    early = k.H[64:P, cols].rearrange("p (s t) -> p s t", t=SEQ)[:, :, 0:SEQ - 1]
    nc.vector.tensor_copy(late, early).then_inc(done, 1)


NU = HEADS * SPC
KW = P + WIN
V_LG, V_LB, V_B2, V_B1A, V_B1G, V_QS, V_KS, V_QSS, V_KSS = 0, 1, 2, 3, 6, 9, 10, 11, 12


def local_layer(k, l, shared):
    here = lambda g: chunk(g - l * NCH)
    G0, G1, L = l * NCH, (l + 1) * NCH, l + 1
    nc, ps = k.nc, k.ps
    with ExitStack() as big:
        names = ["wqkv", "wqks", "wo2", "w1f", "w2f", "vec2"]
        w = {}
        for n in names:
            w[n] = k.sb(f"{n}_{l}", list(k.dram[n].shape)[1:], F32, big)
        with ExitStack() as ctx:
            tab = k.sb(f"tab{l}", [P, 4, CH], ctx=ctx)
            sel = k.sb(f"sel{l}", [P, 2 * NU, P], BF16, ctx)
            hs = k.sb(f"hs{l}", [P, CH], ctx=ctx)
            sq = k.sb(f"sqb{l}", [P, 2, CH], ctx=ctx)
            cl = k.sb(f"cl{l}", [P, 2, CH], ctx=ctx)
            rn = k.sb(f"rn{l}", [P, 2, CH], ctx=ctx)
            ra = k.sb(f"ra{l}", [P, 2, CH], ctx=ctx)
            rb = k.sb(f"rb{l}", [P, 2, CH], ctx=ctx)
            QK = k.sb(f"QK{l}", [P, 2 * NB, CH], ctx=ctx)
            VA = k.sb(f"VA{l}", [P, CH // P, HEADS, 2 * DH], ctx=ctx)
            PT = k.sb(f"PT{l}", [P, 2, KW + P], ctx=ctx)
            OT = k.sb(f"OT{l}", [P, NB, CH], ctx=ctx)
            rd = k.sb(f"rd{l}", [DH, 2, CH], ctx=ctx)
            nm = k.sb(f"nm{l}", [P, 2 * NU], ctx=ctx)
            hl = k.sb(f"hl{l}", [P, P], BF16, ctx)
            mT = k.sb(f"mT{l}", [P, P], BF16, ctx)
            lnb = k.sb(f"lnb{l}", [P, 1], ctx=ctx)
            sem = shared
            (w_in, tab_in, tab_r, zeroed, shifted, proj, v_mm, v_sb, squared, ssq, clipped, logged, rnorm, rotated,
             summed, qk_r, s_mm, max_r, hi_r, hl_r, mT_mm, mT_r, st_mm, pt_r, av_mm, ld_r, rd_r, o_r, x_mm, resid) = map(sem, (
                 "w_in", "tab_in", "tab_r", "zeroed", "shifted", "proj", "v_mm", "v_sb", "squared", "ssq", "clipped",
                 "logged", "rnorm", "rotated", "summed", "qk_r", "s_mm", "max_r", "hi_r", "hl_r", "mT_mm", "mT_r",
                 "st_mm", "pt_r", "av_mm", "ld_r", "rd_r", "o_r", "x_mm", "resid"))
            block = ctx.enter_context(nc.Block())

            @block.sync
            def _(sp):
                for n in names:
                    sp.dma_start(w[n][:], k.dram[n][l]).then_inc(w_in, 16)
                sp.dma_start(tab[:], k.dram["xpos"]).then_inc(tab_in, 16)
                sp.dma_start(sel[:], k.dram["rowsel"]).then_inc(tab_in, 16)

            @block.gpsimd
            def _(pool):
                nc.gpsimd.memset(hs[:], 0.0).then_inc(zeroed, 1)
                nc.gpsimd.memset(VA[:], 1.0).then_inc(zeroed, 1)
                nc.gpsimd.memset(hl[:], 0.0).then_inc(zeroed, 1)
                pool.wait_ge(zeroed, L * 3)
                with pool.Fori(G0, G1) as c:
                    wait_alone(k, pool, av_mm, NU * c + NU)
                    for i in range(2 * NB):
                        wait_alone(k, pool, rotated, 2 * NB * c + i + 3)
                        nc.gpsimd.tensor_tensor(ra[:, i % 2, :], ra[:, i % 2, :], rb[:, i % 2, :], ALU.add).then_inc(summed, 1)
                        wait_alone(k, pool, summed, 2 * NB * c + i + 1)
                        wait_alone(k, pool, rnorm, 2 * NB * c + i + 3)
                        nc.gpsimd.tensor_tensor(QK[:, i, :], ra[:, i % 2, :], rn[:, i % 2, :], ALU.mult).then_inc(qk_r, 1)

            @block.tensor
            def _(pe):
                if l == 0:
                    pe.sem_inc(v_mm, 4)
                if l == 0:
                    pe.sem_inc(av_mm, NU)
                pe.wait_ge(w_in, L * 16 * len(names))
                pe.wait_ge(tab_in, L * 32)
                pe.wait_ge(zeroed, L * 3)
                with pe.Fori(G0, G1) as c:
                    pe.wait_ge(shifted, c + 1)
                    pe.wait_ge(pt_r, NU * c + 2)
                    for i in range(2 * NB + 1):
                        if i < 2 * NB:
                            pe.wait_ge(rotated, 2 * NB * c + i + 1)
                            if i < 2:
                                pe.wait_ge(max_r, NU * c + i + 1)
                            nc.tensor.matmul(ps[i % 2][:], w["wqkv"][:, i * P:(i + 1) * P], hs[:], start=True, stop=True)
                            nc.tensor.matmul(ps[2 + i % 2][:], w["wqks"][:, i * P:(i + 1) * P], hs[:],
                                             start=True, stop=True).then_inc(proj, 1)
                        if i > 0:
                            j = i - 1
                            pe.wait_ge(squared, 2 * NB * c + j + 1)
                            pe.wait_ge(clipped, 2 * NB * c + j + 1)
                            if j == 1:
                                pe.wait_ge(o_r, HEADS * c + 2)
                            nc.tensor.matmul(ps[4 + j % 2][:], k.const["headmean"][:], sq[:, j % 2, :],
                                             start=True, stop=True).then_inc(ssq, 1)
                    for t in range(CH // P):
                        pe.wait_ge(v_sb, 4 * c + t + 1)
                        nc.tensor.matmul(ps[6 + t % 2][:], hs[:, t * P:(t + 1) * P], w["wqkv"][:, 2 * INNER:3 * INNER],
                                         start=True, stop=True).then_inc(v_mm, 1)
                    pe.wait_ge(qk_r, 2 * NB * (c + 1))
                    for u in range(NU):
                        h, s = u // SPC, u % SPC
                        r, b, o = DH * (h % 2), h // 2, s * SEQ
                        if u >= 2:
                            pe.wait_ge(max_r, NU * c + u + 1)
                        nc.tensor.matmul(ps[u % 2][:, 0:2 * KW], k.const["identb"][:], k.const["mask_q"][:], start=True, stop=False)
                        nc.tensor.matmul(ps[u % 2][:, WIN:KW], QK[r:r + DH, b, o:o + P], QK[r:r + DH, NB + b, o:o + P],
                                         start=False, stop=False)
                        nc.tensor.matmul(ps[u % 2][:, KW:2 * KW], QK[r:r + DH, b, o + P:o + SEQ],
                                         QK[r:r + DH, NB + b, o + WIN:o + SEQ], start=False, stop=True).then_inc(s_mm, 1)
                    wait_alone(k, pe, hl_r, c + 1)
                    nc.tensor.transpose(ps[2][:].bitcast(BF16)[:, 0:P], hl[:], k.const["identb"][:]).then_inc(mT_mm, 1)
                    pe.wait_ge(mT_r, c + 1)
                    pe.wait_ge(v_sb, 4 * c + 6)
                    for u in range(NU + 1):
                        if u < NU:
                            h, s = u // SPC, u % SPC
                            r, b, o = DH * (h % 2), h // 2, s * SEQ
                            bank = ps[3 + u % 2]
                            if u >= 2:
                                pe.wait_ge(pt_r, NU * c + u + 1)
                            q, key = QK[r:r + DH, b, :], QK[r:r + DH, NB + b, :]
                            nc.tensor.matmul(bank[:, 0:KW + P], k.const["identb"][:], k.const["mask_k"][:], start=True, stop=False)
                            nc.tensor.matmul(bank[:, 0:KW], key[:, o:o + P], q[:, o:o + KW], start=False, stop=False)
                            nc.tensor.matmul(bank[:, KW:KW + P], key[:, o + P:o + SEQ], q[:, o + P:o + SEQ],
                                             start=False, stop=False)
                            nc.tensor.matmul(bank[:, 0:P], sel[:, 2 * u, :], mT[:], start=False, stop=False)
                            nc.tensor.matmul(bank[:, P:KW], sel[:, 2 * u + 1, :], mT[:, 0:WIN], start=False, stop=False)
                            nc.tensor.matmul(bank[:, KW:KW + P], sel[:, 2 * u + 1, :], mT[:],
                                             start=False, stop=True).then_inc(st_mm, 1)
                        if u > 0:
                            h, s = (u - 1) // SPC, (u - 1) % SPC
                            o = s * SEQ
                            if s == 0 :
                                pe.wait_ge(o_r, HEADS * c + h + 1)
                            pe.wait_ge(pt_r, NU * c + u + 2)
                            pt = PT[:, (u - 1) % 2, :]
                            nc.tensor.matmul(ps[5 + h % 2][:, o:o + KW], VA[:, 2 * s, h, :], pt[:, 0:KW],
                                             start=True, stop=False)
                            nc.tensor.matmul(ps[5 + h % 2][:, o + P:o + KW], VA[:, 2 * s + 1, h, :], pt[:, KW:KW + WIN],
                                             start=False, stop=True)
                            nc.tensor.matmul(ps[5 + h % 2][:, o + KW:o + SEQ], VA[:, 2 * s + 1, h, :],
                                             pt[:, KW + WIN:KW + P], start=True, stop=True).then_inc(av_mm, 1)
                    pe.wait_ge(o_r, HEADS * (c + 1) + 2)
                    for b in range(NB):
                        i = nc.tensor.matmul(ps[7][:], w["wo2"][:, b, :], OT[:, b, :], start=(b == 0), stop=(b == NB - 1))
                    i.then_inc(x_mm, 1)
                    pe.wait_ge(resid, c + 1)

            @block.scalar
            def _(act):
                nc.scalar.preload_act_table_set(LNEXP)
                if l == 0:
                    act.sem_inc(rnorm, 2)
                if l == 0:
                    act.sem_inc(v_sb, 2)
                if l == 0:
                    act.sem_inc(pt_r, 2)
                if l == 0:
                    act.sem_inc(rd_r, 2)
                act.wait_ge(zeroed, L * 3)
                act.wait_ge(tab_r, L * 5)
                with act.Fori(G0, G1) as c:
                    for i in range(2 * NB + 1):
                        if i < 2 * NB:
                            act.wait_ge(proj, 2 * NB * c + i + 1)
                            nc.scalar.activation(sq[:, i % 2, :], ps[i % 2][:], ACT.Square).then_inc(squared, 1)
                        if i > 0:
                            j = i - 1
                            act.wait_ge(clipped, 2 * NB * c + j + 3)
                            nc.scalar.activation(cl[:, j % 2, :], cl[:, j % 2, :], ACT.Ln,
                                                 scale=float(2 ** LN_SHIFT)).then_inc(logged, 1)
                            act.wait_ge(logged, 2 * NB * c + j + 1)
                            if j >= 2:
                                act.wait_ge(qk_r, 2 * NB * c + j - 1)
                            nc.scalar.activation(rn[:, j % 2, :], cl[:, j % 2, :], ACT.Exp, scale=-0.5,
                                                 bias=lnb[:, 0:1]).then_inc(rnorm, 1)
                    for t in range(CH // P):
                        act.wait_ge(v_mm, 4 * c + t + 5)
                        act.wait_ge(av_mm, NU * c + NU)
                        nc.scalar.activation(VA[:, t, :, 0:DH], ps[6 + t % 2][:].rearrange("p (h d) -> p h d", d=DH),
                                             ACT.Copy).then_inc(v_sb, 1)
                    act.wait_ge(mT_mm, c + 1)
                    nc.scalar.activation(mT[:], ps[2][:].bitcast(BF16)[:, 0:P], ACT.Copy).then_inc(mT_r, 1)
                    for u in range(NU + 1):
                        if u < NU:
                            act.wait_ge(st_mm, NU * c + u + 1)
                            act.wait_ge(av_mm, NU * c + u - 1 + NU)
                            nc.scalar.activation(PT[:, u % 2, :], ps[3 + u % 2][:, 0:KW + P], ACT.Exp,
                                                 scale=QK_SCALE).then_inc(pt_r, 1)
                        if u > 0 and u % SPC == 0:
                            h = u // SPC - 1
                            act.wait_ge(av_mm, NU * c + u + NU)
                            act.wait_ge(o_r, HEADS * c + h + 1)
                            nc.scalar.activation(rd[:, h % 2, :], ps[5 + h % 2][DH:P, :], ACT.Ln).then_inc(ld_r, 1)
                            act.wait_ge(ld_r, HEADS * c + h + 1)
                            nc.scalar.activation(rd[:, h % 2, :], rd[:, h % 2, :], ACT.Exp, scale=-1.0).then_inc(rd_r, 1)

            @block.vector
            def _(dve):
                if l == 0:
                    dve.sem_inc(rotated, 2)
                if l == 0:
                    dve.sem_inc(clipped, 2)
                if l == 0:
                    dve.sem_inc(max_r, 2)
                if l == 0:
                    dve.sem_inc(o_r, 2)
                nc.vector.memset(lnb[:], 0.5 * LN_SHIFT * 0.6931471805599453).then_inc(tab_r, 1)
                dve.wait_ge(w_in, L * 16 * len(names))
                dve.wait_ge(tab_in, L * 32)
                for i, col in enumerate((V_QS, V_QSS, V_KS, V_KSS)):
                    nc.vector.tensor_scalar(tab[:, i, :], tab[:, i, :], w["vec2"][:, col:col + 1], None,
                                            ALU.mult).then_inc(tab_r, 1)
                dve.wait_ge(tab_r, L * 5)
                dve.wait_ge(zeroed, L * 3)
                with dve.Fori(G0, G1) as c:
                    dve.wait_ge(v_mm, 4 * c + 4)
                    shift_tokens(k, shifted, hs, here(c))
                    for i in range(2 * NB + 1):
                        if i < 2 * NB:
                            t = 0 if i < NB else 2
                            dve.wait_ge(proj, 2 * NB * c + i + 1)
                            if i >= 2:
                                dve.wait_ge(qk_r, 2 * NB * c + i - 1)
                            nc.vector.tensor_tensor(rb[:, i % 2, :], ps[2 + i % 2][:], tab[:, t + 1, :], ALU.mult)
                            dve.wait_ge(squared, 2 * NB * c + i + 1)
                            nc.vector.tensor_tensor(ra[:, i % 2, :], ps[i % 2][:], tab[:, t, :],
                                                    ALU.mult).then_inc(rotated, 1)
                        if i > 0:
                            j = i - 1
                            dve.wait_ge(ssq, 2 * NB * c + j + 1)
                            dve.wait_ge(rnorm, 2 * NB * c + j + 1)
                            nc.vector.tensor_scalar(cl[:, j % 2, :], ps[4 + j % 2][:], CLIP2, None, ALU.max).then_inc(clipped, 1)
                    for u in range(NU):
                        dve.wait_ge(s_mm, NU * c + u + 1)
                        nc.vector.tensor_reduce(nm[:, 2 * u:2 * u + 2],
                                                ps[u % 2][:, 0:2 * KW].rearrange("p (a b) -> p a b", a=2),
                                                AX.X, ALU.max, negate=True).then_inc(max_r, 1)
                    dve.wait_ge(max_r, NU * (c + 1) + 2)
                    nc.vector.tensor_copy(hl[:, 0:2 * NU], nm[:]).then_inc(hi_r, 1)
                    dve.wait_ge(hi_r, c + 1)
                    nc.vector.tensor_tensor(hl[:, 2 * NU:4 * NU], nm[:], hl[:, 0:2 * NU], ALU.subtract).then_inc(hl_r, 1)
                    for h in range(HEADS):
                        r = DH * (h % 2)
                        dve.wait_ge(rd_r, HEADS * c + h + 3)
                        nc.vector.tensor_tensor(OT[r:r + DH, h // 2, :], ps[5 + h % 2][0:DH, :], rd[:, h % 2, :],
                                                ALU.mult).then_inc(o_r, 1)
                    dve.wait_ge(x_mm, c + 1)
                    nc.vector.tensor_tensor(k.H[:, here(c)], ps[7][:], k.H[:, here(c)], ALU.add).then_inc(resid, 1)

        with ExitStack() as ctx:
            hs = k.sb(f"hsf{l}", [P, CH], ctx=ctx)
            hn = k.sb(f"hn{l}", [P, CH], ctx=ctx)
            Gg = k.sb(f"Gg{l}", [P, NHB, CH], ctx=ctx)
            U = k.sb(f"Uf{l}", [P, NHB, CH], ctx=ctx)
            b = ln_buffers(k, ctx, f"nf{l}", 6, 7)
            s = LnSems(*(shared(f"nf_{n}") for n in LnSems._fields))
            sem = shared
            zeroed, shifted, affine, a_mm, g_mm, gelu, u_r, x_mm, resid = map(sem, (
                "zeroedf", "shiftedf", "affinef", "a_mm", "g_mm", "geluf", "u_r", "xf_mm", "residf"))
            block = ctx.enter_context(nc.Block())

            @block.gpsimd
            def _(pool):
                nc.gpsimd.memset(hs[:], 0.0).then_inc(zeroed, 1)

            @block.tensor
            def _(pe):
                with pe.Fori(G0, G1) as c:
                    pe.wait_ge(shifted, c + 1)
                    ln_centre(k, pe, s, b, c + 1, hs[:])
                    ln_variance(k, pe, s, b, c + 1)
                    pe.wait_ge(affine, c + 1)
                    pe.wait_ge(resid, c + 1)
                    for j in range(NHB):
                        n = hid_rows(j)
                        nc.tensor.matmul(ps[3 + j][0:n, :], w["w1f"][:, HID + j * P:HID + j * P + n], hn[:],
                                         start=True, stop=True).then_inc(g_mm, 1)
                    for j in range(NHB):
                        n = hid_rows(j)
                        nc.tensor.matmul(ps[j][0:n, :], w["w1f"][:, j * P:j * P + n], hn[:],
                                         start=True, stop=True).then_inc(a_mm, 1)
                    pe.wait_ge(u_r, NHB * (c + 1))
                    for j in range(NHB):
                        n = hid_rows(j)
                        i = nc.tensor.matmul(ps[0][:], w["w2f"][0:n, j, :], U[0:n, j, :], start=(j == 0), stop=(j == NHB - 1))
                    i.then_inc(x_mm, 1)

            @block.scalar
            def _(act):
                with act.Fori(G0, G1) as c:
                    nc.scalar.preload_act_table_set(LNEXP)
                    ln_rstd(k, act, s, b, c + 1)
                    for j in range(NHB):
                        n = hid_rows(j)
                        act.wait_ge(g_mm, NHB * c + j + 1)
                        nc.scalar.activation(Gg[0:n, j, :], ps[3 + j][0:n, :], ACT.Gelu,
                                             bias=w["vec2"][0:n, V_B1G + j:V_B1G + j + 1]).then_inc(gelu, 1)

            @block.vector
            def _(dve):
                if l == 0:
                    dve.sem_inc(s.normed, 1)
                if l == 0:
                    dve.sem_inc(resid, 1)
                dve.wait_ge(zeroed, L)
                with dve.Fori(G0, G1) as c:
                    shift_tokens(k, shifted, hs, here(c))
                    ln_scale(k, dve, s, b, c + 1, hn[:])
                    dve.wait_ge(s.normed, c + 2)
                    nc.vector.tensor_scalar(hn[:], hn[:], w["vec2"][:, V_LG:V_LG + 1], w["vec2"][:, V_LB:V_LB + 1],
                                            ALU.mult, ALU.add).then_inc(affine, 1)
                    for j in range(NHB):
                        n = hid_rows(j)
                        dve.wait_ge(a_mm, NHB * c + j + 1)
                        dve.wait_ge(gelu, NHB * c + j + 1)
                        nc.vector.scalar_tensor_tensor(U[0:n, j, :], ps[j][0:n, :], w["vec2"][0:n, V_B1A + j:V_B1A + j + 1],
                                                       Gg[0:n, j, :], ALU.add, ALU.mult).then_inc(u_r, 1)
                    dve.wait_ge(x_mm, c + 1)
                    nc.vector.scalar_tensor_tensor(k.H[:, here(c)], ps[0][:], w["vec2"][:, V_B2:V_B2 + 1],
                                                   k.H[:, here(c)], ALU.add, ALU.add).then_inc(resid, 1)


def build(nc, dram, out, stages=None):
    with ExitStack() as ctx:
        k = Kernel(nc, dram, out, ctx)
        load(k)
        norm_stage(k, "n0")
        linear_attention(k)
        experts(k)
        retention(k)
        sems = {}

        def shared(name):
            if name not in sems:
                sems[name] = ctx.enter_context(nc.semaphore(name))
            return sems[name]

        norm_stage(k, "n4")
        for l in range(DEPTH):
            local_layer(k, l, shared)
        store(k)


def constants():
    import numpy as np

    f, bf = np.float32, np.dtype("bfloat16")
    eye = np.eye(P, dtype=f)
    c = {"ident": eye, "centre": eye - f(1 / P), "mean": np.full((P, P), 1 / P, f), "identb": eye.astype(bf)}
    c["headmean"] = np.kron(np.eye(P // DH), np.ones((DH, DH))).astype(f)
    i = np.arange(P)[:, None]
    low = -1e30
    j = np.arange(KW)[None, :]
    q0 = (j - WIN >= 0) & (j - WIN <= i) & (j - WIN >= i - WIN)
    q1 = (WIN + j <= P + i) & (WIN + j >= P + i - WIN)
    c["mask_q"] = np.where(np.concatenate([q0, q1], 1), 0, low).astype(bf)
    k0 = (i <= j) & (j <= i + WIN)
    c["mask_k"] = np.where(np.concatenate([k0, k0[:, :P]], 1), 0, low).astype(bf)
    rows = np.zeros((P, 2 * NU, P), f)
    for r in range(2 * NU):
        rows[r, r] = rows[2 * NU + r, r] = 1
    c["rowsel"] = rows.astype(bf)
    half = D0 // 2
    inv = f(1) / np.power(f(10000), np.arange(half, dtype=f) / f(half))
    fr = np.arange(SEQ, dtype=f)[:, None] * inv
    d = np.arange(P) % D0
    cos, sin = np.cos(fr).astype(f)[:, d % half].T, np.sin(fr).astype(f)[:, d % half].T
    sin = sin * np.where(d < half, -1, 1).astype(f)[:, None]
    c["rope0"] = np.stack([np.tile(cos, SPC), np.tile(sin, SPC)], 1)
    spread = np.zeros((P, D0, P), f)
    for dd in range(D0):
        for o in range(P):
            spread[o // D0 * D0 + dd, dd, o] = 1
    c["spread"] = spread
    c["headsum"] = np.kron(np.eye(NH0), np.ones((D0, D0))).astype(f)
    c["iota8"] = np.tile(np.arange(NE, dtype=f) - NE, (P, NT, 1))
    c["tri"] = np.triu(np.ones((P, P))).astype(bf)
    c["ones"] = np.ones((P, P), bf)
    pick = np.zeros((P, NX, P), f)
    for e in range(NX):
        pick[e:NPART * NX:NX, e] = 1
    c["pick"] = pick.reshape(P, NX * P).astype(bf)
    hi = np.arange(0, DH, 2, dtype=f)
    inv = f(1) / np.power(f(10000), hi / f(DH))
    t = np.arange(SEQ, dtype=f)
    fr = t[:, None] * inv[None, :]
    base = (hi + f(0.4 * DH)) / f(1.4 * DH)
    scale = np.power(base[None, :], ((t - SEQ // 2) / f(WIN // 2))[:, None])
    d = np.arange(P) % DH
    cs, sn, sc = (a[:, d % (DH // 2)].T.astype(f) for a in (np.cos(fr), np.sin(fr), scale))
    sn = sn * np.where(d < DH // 2, -1, 1).astype(f)[:, None]
    c["xpos"] = np.stack([np.tile(a, SPC) for a in (cs * sc, sn * sc, cs / sc, sn / sc)], 1).astype(f)
    return {n: np.ascontiguousarray(a) for n, a in c.items()}


def layouts(a):
    import numpy as np

    g = {n: np.asarray(v) for n, v in a.items()}
    r = {"x": g["L0_attn_x"]}
    o = np.arange(P)
    swap0 = o // D0 * D0 + (o % D0 + D0 // 2) % D0
    for n, s in (("q", "L0_attn_Wq"), ("k", "L0_attn_Wk")):
        r[f"w{n}0"] = g[s].T
        r[f"w{n}0s"] = g[s][swap0].T
    r["wv0"] = g["L0_attn_Wv"].T
    per_row = lambda v, m: v[o // D0 * M0 + m]
    r["wbeta"] = np.stack([per_row(g["L0_attn_Wbeta"], m).T for m in range(M0)], 1)
    r["wmix"] = np.stack([per_row(g["L0_attn_Wmix"], m).T for m in range(M0)], 1)
    r["wout0"] = g["L0_attn_Wout"].T
    r["vec0"] = np.stack([per_row(g[n], m) for n in ("L0_attn_bbeta", "L0_attn_bmix") for m in range(M0)]
                         + [g["L0_attn_bout"], g["L0_attn_ln_g"], g["L0_attn_ln_b"]], 1)
    r["wr"] = g["L0_ffn_Wr"].T
    add = lambda x, y: np.concatenate([x, y[None]], 0)
    r["w1e"] = add(g["L0_ffn_W1"], g["L0_ffn_fw1"]).transpose(1, 0, 2)
    r["w2e"] = add(g["L0_ffn_W2"], g["L0_ffn_fw2"]).reshape(NX, NJ, P, P).transpose(2, 0, 1, 3)
    r["b1e"] = add(g["L0_ffn_b1"], g["L0_ffn_fb1"]).reshape(NX, NJ, P).transpose(2, 0, 1)
    r["b2e"] = add(g["L0_ffn_b2"], g["L0_ffn_fb2"]).T
    for n in "qvgo":
        r[f"w{n}1"] = g[f"L1_attn_W{n}"].T
    r["vec1"] = np.stack([np.repeat(g["L1_attn_decay"], P // 16), g["L1_attn_ln_gamma"], g["L1_attn_ln_beta"]], 1)
    r["wqkv"] = g["L1_ffn_wqkv"]
    i = np.arange(2 * INNER)
    r["wqks"] = g["L1_ffn_wqkv"][:, :, i // DH * DH + (i % DH + DH // 2) % DH]
    r["wo2"] = g["L1_ffn_wo"].reshape(DEPTH, NB, P, P).transpose(0, 2, 1, 3)
    r["w1f"] = g["L1_ffn_w1"]
    pad = lambda v, n: np.concatenate([v, np.zeros((v.shape[0], n - v.shape[1]) + v.shape[2:], v.dtype)], 1)
    r["w2f"] = pad(g["L1_ffn_w2"], NHB * P).reshape(DEPTH, NHB, P, P).transpose(0, 2, 1, 3)
    cols = [g["L1_ffn_ln_g"], g["L1_ffn_ln_b"], g["L1_ffn_b2"]]
    for lo in (0, HID):
        v = pad(g["L1_ffn_b1"][:, lo:lo + HID], NHB * P)
        cols += [v[:, j * P:(j + 1) * P] for j in range(NHB)]
    d = np.arange(P) % DH
    ds = (d + DH // 2) % DH
    cols += [g["L1_ffn_q_scale"][:, d], g["L1_ffn_k_scale"][:, d], g["L1_ffn_q_scale"][:, ds], g["L1_ffn_k_scale"][:, ds]]
    r["vec2"] = np.stack(cols, 2)
    return {n: np.ascontiguousarray(v) for n, v in r.items()}


def kernel(**inputs):
    import concourse.bacc as _bacc
    from concourse.bass_utils import run_bass_kernel_spmd as _run

    nc = _bacc.Bacc("TRN2", target_bir_lowering=False, num_devices=1)
    arrays = {**constants(), **layouts(inputs)}
    dram = {n: nc.dram_tensor(f"{n}_dram", v.shape, mybir.dt.from_np(v.dtype), kind="ExternalInput").ap()
            for n, v in arrays.items()}
    out = nc.dram_tensor("out_dram", (NSEQ, SEQ, P), F32, kind="ExternalOutput").ap()
    build(nc, dram, out)
    r = _run(nc, [{f"{n}_dram": v for n, v in arrays.items()}], core_ids=[0])
    return r.results[0]["out_dram"]
```

```python
from collections import namedtuple
from contextlib import ExitStack

import concourse.bass as bass
from concourse import mybir

F32 = mybir.dt.float32
BF16 = mybir.dt.bfloat16
F32R = mybir.dt.float32r
ALU = mybir.AluOpType
ACT = mybir.ActivationFunctionType
AX = mybir.AxisListType

P = 128
NSEQ, SEQ = 16, 256
T = NSEQ * SEQ
CH = 512
NCH = T // CH
SPC = CH // SEQ
NT = T // P
LN_EPS = 1e-5

NH0, D0, M0 = 32, 4, 2
BMIN, BMAX, DEN_EPS = 0.85, 0.9995, 1e-6
NE = 8
CAP = int(1.25 * (T * 2 / NE))
FFI = 512
NJ = FFI // P
NX = NE + 1
NPART = 3
DEPTH, HEADS, DH, WIN = 2, 8, 64, 64
INNER = HEADS * DH
NB = INNER // P
HID = 341
QK_SCALE = 8.0
LNEXP = "natural_log_exp_and_others"
CLIP2 = 1e-24
LN_SHIFT = 18


PASSES = ((0, 0), (0, 1), (1, 0))


def hid_rows(j):
    return min(P, HID - j * P)


NHB = (HID + P - 1) // P


def chunk(c):
    return bass.ds(c * CH, CH)


class Kernel:

    def __init__(self, nc, dram, out, ctx):
        self.nc, self.dram, self.out, self.ctx = nc, dram, out, ctx
        self.started, self.turned, self.stored, self.weights_in = (
            ctx.enter_context(nc.semaphore(n)) for n in ("started", "tiles_turned", "tiles_stored", "weights_in"))
        self.w_hi, self.w_lo, self.late_in = (ctx.enter_context(nc.semaphore(n)) for n in ("w_hi", "w_lo", "late_in"))
        self.ps = [ctx.enter_context(nc.psum_tensor(f"bank{i}", [P, CH], F32)) for i in range(8)]

    def sb(self, name, shape, dt=F32, ctx=None):
        return (ctx or self.ctx).enter_context(self.nc.sbuf_tensor(name, shape, dt))


def wait_alone(k, eng, sem, value):
    if not isinstance(value, int):
        value = eng.snap(value)
    eng.wait_ge(k.started, 1)
    eng.wait_ge(sem, value)


LnSems = namedtuple("LnSems", "centred squared var logged rstd normed")
LnBuffers = namedtuple("LnBuffers", "sq lg rs x v")


def ln_sems(nc, ctx, name):
    return LnSems(*(ctx.enter_context(nc.semaphore(f"{name}_{n}")) for n in LnSems._fields))


def ln_buffers(k, ctx, name, bank_x, bank_v):
    return LnBuffers(sq=k.sb(f"{name}_sq", [P, CH], ctx=ctx), lg=k.sb(f"{name}_lg", [P, CH], ctx=ctx),
                           rs=k.sb(f"{name}_rs", [P, CH], ctx=ctx), x=k.ps[bank_x], v=k.ps[bank_v])


def ln_centre(k, pe, s, b, n, src):
    pe.wait_ge(s.normed, n)
    k.nc.tensor.matmul(b.x[:], k.const["centre"][:], src, start=True, stop=True).then_inc(s.centred, 1)


def ln_variance(k, pe, s, b, n):
    pe.wait_ge(s.squared, n)
    k.nc.tensor.matmul(b.v[:], k.const["mean"][:], b.sq[:], start=True, stop=True).then_inc(s.var, 1)


def ln_square(k, act, s, b, n):
    act.wait_ge(s.centred, n)
    k.nc.scalar.activation(b.sq[:], b.x[:], ACT.Square).then_inc(s.squared, 1)


def ln_rstd(k, act, s, b, n):
    act.wait_ge(s.var, n)
    k.nc.scalar.activation(b.lg[:], b.v[:], ACT.Ln, bias=k.eps[:, 0:1]).then_inc(s.logged, 1)
    act.wait_ge(s.logged, n)
    k.nc.scalar.activation(b.rs[:], b.lg[:], ACT.Exp, scale=-0.5).then_inc(s.rstd, 1)


def ln_scale(k, dve, s, b, n, dst):
    dve.wait_ge(s.rstd, n)
    k.nc.vector.tensor_tensor(dst, b.x[:], b.rs[:], ALU.mult).then_inc(s.normed, 1)


ROUTING = ["wr", "iota8", "tri", "ones"]
RETENTION = ["wq1", "wv1", "wg1", "wo1", "vec1"]
CONSTS = ["ident", "centre", "mean", "identb", "headmean", "mask_q", "mask_k", *ROUTING, *RETENTION]
N_FIRST = 7
WEIGHTS0 = ["wq0", "wq0s", "wk0", "wk0s", "wv0", "wbeta", "wmix", "wout0", "vec0", "rope0", "spread", "headsum"]
N_LATE = len(CONSTS) - N_FIRST


def residents(k):
    k.XT = k.sb("XT", [P, T])
    k.H = k.sb("H", [P, T + CH])
    k.const = {}
    k.eps = k.sb("eps", [P, 1])
    for n in CONSTS:
        v = k.dram[n]
        k.const[n] = k.sb(n, list(v.shape), v.dtype)


def load(k):
    nc = k.nc
    xf = k.dram["x"].rearrange("b t d -> (b t) d").rearrange("(n p) d -> p n d", p=P)
    with ExitStack() as ctx:
        tok = k.sb("tok", [P, NT, P], ctx=ctx)
        sem = lambda n: ctx.enter_context(nc.semaphore(n))
        const_in = sem("const_in")
        x_in = [sem(f"x_in{q}") for q in range(NCH // 4)]
        turned, stored = k.turned, k.stored
        block = ctx.enter_context(nc.Block())

        @block.sync
        def _(sp):
            sp.dma_start(k.const["ident"][:], k.dram["ident"]).then_inc(x_in[0], 16)
            for q in range(NCH):
                sp.dma_start(tok[:, 4 * q:4 * q + 4, :], xf[:, 4 * q:4 * q + 4, :]).then_inc(x_in[q // 4], 16)
            for n in CONSTS[1:N_FIRST]:
                sp.dma_start(k.const[n][:], k.dram[n]).then_inc(const_in, 16)

        @block.tensor
        def _(pe):
            for n in range(NT):
                if n % 16 == 0:
                    pe.wait_ge(x_in[n // 16], 16 * (4 + (n == 0)))
                if n % 4 == 0 and n >= 8:
                    pe.wait_ge(stored, n // 4 - 1)
                t = nc.tensor.transpose(k.ps[(n // 4) % 2][:, (n % 4) * P:(n % 4 + 1) * P], tok[:, n, :], k.const["ident"][:])
                if n % 4 == 3:
                    t.then_inc(turned, 1)

        @block.scalar
        def _(act):
            for q in range(NCH):
                act.wait_ge(turned, q + 1)
                nc.scalar.activation(k.XT[:, q * CH:(q + 1) * CH], k.ps[q % 2][:], ACT.Copy).then_inc(stored, 1)

        @block.vector
        def _(dve):
            nc.vector.memset(k.H[:, T:T + CH], 0.0)
            nc.vector.memset(k.eps[:], LN_EPS).then_inc(k.started, 1)
            dve.wait_ge(k.started, 1)

        @block.gpsimd
        def _(pool):
            pool.wait_ge(const_in, 16 * (N_FIRST - 1))


def store(k):
    nc = k.nc
    of = k.out.rearrange("b t d -> (b t) d").rearrange("(n p) d -> p n d", p=P)
    with ExitStack() as ctx:
        tok = k.sb("tok_out", [P, NT, P], ctx=ctx)
        sem = lambda n: ctx.enter_context(nc.semaphore(n))
        total, written = map(sem, ("total", "y_written"))
        turned, copied = k.turned, k.stored
        block = ctx.enter_context(nc.Block())

        @block.vector
        def _(dve):
            for q in range(NCH):
                cols = slice(q * CH, (q + 1) * CH)
                nc.vector.tensor_tensor(k.XT[:, cols], k.XT[:, cols], k.H[:, cols], ALU.add).then_inc(total, 1)

        @block.tensor
        def _(pe):
            for n in range(NT):
                pe.wait_ge(total, n // 4 + 1)
                if n % 4 == 0 and n >= 8:
                    pe.wait_ge(copied, NCH + n // 4 - 1)
                t = nc.tensor.transpose(k.ps[(n // 4) % 2][:, (n % 4) * P:(n % 4 + 1) * P],
                                        k.XT[:, n * P:(n + 1) * P], k.const["ident"][:])
                if n % 4 == 3:
                    t.then_inc(turned, 1)

        @block.scalar
        def _(act):
            for q in range(NCH):
                act.wait_ge(turned, NCH + q + 1)
                nc.scalar.activation(tok[:, 4 * q:4 * q + 4, :], k.ps[q % 2][:].rearrange("p (a b) -> p a b", a=4),
                                     ACT.Copy).then_inc(copied, 1)

        @block.sync
        def _(sp):
            for q in range(NCH):
                sp.wait_ge(copied, NCH + q + 1)
                sp.dma_start(of[:, 4 * q:4 * q + 4, :], tok[:, 4 * q:4 * q + 4, :]).then_inc(written, 16)
            sp.wait_ge(written, 16 * NCH)


def norm_stage(k, name, base, s, w0=None):
    nc, W = k.nc, 4
    with ExitStack() as ctx:
        b = [ln_buffers(k, ctx, f"{name}_{i}", i, 4 + i) for i in range(W)]
        block = ctx.enter_context(nc.Block())

        @block.sync
        def _(sp):
            for n in w0 or ():
                sp.dma_start(w0[n][:], k.dram[n]).then_inc(k.weights_in, 16)

        @block.tensor
        def _(pe):
            with pe.Fori(base // W, (base + NCH) // W) as c:
                for i in range(W):
                    ln_centre(k, pe, s, b[i], W * c + i + 1, k.XT[:, chunk(W * c + i - base)])
                for i in range(W):
                    ln_variance(k, pe, s, b[i], W * c + i + 1)

        @block.scalar
        def _(act):
            nc.scalar.preload_act_table_set(LNEXP)
            with act.Fori(base // W, (base + NCH) // W) as c:
                for i in range(W):
                    ln_square(k, act, s, b[i], W * c + i + 1)
                for i in range(W):
                    ln_rstd(k, act, s, b[i], W * c + i + 1)

        @block.vector
        def _(dve):
            if base == 0:
                dve.sem_inc(s.normed, W)
            with dve.Fori(base // W, (base + NCH) // W) as c:
                for i in range(W):
                    ln_scale(k, dve, s, b[i], W * c + i + 1, k.H[:, chunk(W * c + i - base)])


def linear_attention(k, w):
    nc, ps = k.nc, k.ps
    with ExitStack() as big:
        beta = [k.sb(f"beta{m}", [P, T], ctx=big) for m in range(M0)]
        mix = [k.sb(f"mix{m}", [P, T], ctx=big) for m in range(M0)]
        Y = k.sb("Y0", [P, T], ctx=big)
        wmixd = k.sb("wmixd", [P, P], ctx=big)
        bd = k.sb("bmixd", [P, 2], ctx=big)
        with ExitStack() as ctx:
            sem = lambda n: ctx.enter_context(nc.semaphore(n))
            diff, logits, gates, clipped = map(sem, ("mix_diff", "gate_logits", "gate_values", "beta_clipped"))
            block = ctx.enter_context(nc.Block())

            @block.sync
            def _(sp):
                for n in CONSTS[N_FIRST:]:
                    sp.dma_start(k.const[n][:], k.dram[n]).then_inc(k.late_in, 16)

            @block.tensor
            def _(pe):
                pe.wait_ge(k.weights_in, 16 * len(WEIGHTS0))
                pe.wait_ge(diff, 3)
                with pe.Fori(0, NCH // 2) as c2:
                    for i in range(2):
                        c, bank = 2 * c2 + i, 4 * i
                        pe.wait_ge(gates, c * 4 + 4)
                        for m in range(M0):
                            nc.tensor.matmul(ps[bank + m][:], w["wbeta"][:, m, :], k.H[:, chunk(c)], start=True, stop=True)
                        nc.tensor.matmul(ps[bank + 2][:], wmixd[:], k.H[:, chunk(c)], start=True, stop=True).then_inc(logits, 1)

            @block.scalar
            def _(act):
                act.sem_inc(gates, 8)
                nc.scalar.preload_act_table(ACT.Sigmoid)
                act.wait_ge(k.weights_in, 16 * len(WEIGHTS0))
                act.wait_ge(diff, 3)
                with act.Fori(0, NCH // 2) as c2:
                    for i in range(2):
                        c, bank = 2 * c2 + i, 4 * i
                        act.wait_ge(logits, c + 1)
                        for m in range(M0):
                            nc.scalar.activation(beta[m][:, chunk(c)], ps[bank + m][:], ACT.Sigmoid,
                                                 bias=w["vec0"][:, m:m + 1]).then_inc(gates, 1)
                        nc.scalar.activation(mix[0][:, chunk(c)], ps[bank + 2][:], ACT.Sigmoid, bias=bd[:, 0:1]).then_inc(gates, 1)
                        nc.scalar.activation(mix[1][:, chunk(c)], ps[bank + 2][:], ACT.Sigmoid, bias=bd[:, 1:2],
                                             scale=-1.0).then_inc(gates, 1)

            @block.vector
            def _(dve):
                dve.wait_ge(k.weights_in, 16 * len(WEIGHTS0))
                nc.vector.tensor_tensor(wmixd[:], w["wmix"][:, 0, :], w["wmix"][:, 1, :], ALU.subtract).then_inc(diff, 1)
                nc.vector.tensor_tensor(bd[:, 0:1], w["vec0"][:, 2:3], w["vec0"][:, 3:4], ALU.subtract).then_inc(diff, 1)
                nc.vector.tensor_tensor(bd[:, 1:2], w["vec0"][:, 3:4], w["vec0"][:, 2:3], ALU.subtract).then_inc(diff, 1)
                with dve.Fori(0, NCH) as c:
                    dve.wait_ge(gates, c * 4 + 10)
                    for m in range(M0):
                        nc.vector.tensor_scalar(beta[m][:, chunk(c)], beta[m][:, chunk(c)], BMIN, BMAX,
                                                ALU.max, ALU.min).then_inc(clipped, 1)
                dve.wait_ge(clipped, 2 * NCH)
                for m in range(M0):
                    nc.vector.memset(beta[m][:].rearrange("p (s t) -> p s t", t=SEQ)[:, :, 0:1], 0.0)

        with ExitStack() as ctx:
            buf = lambda n: k.sb(n, [P, CH], ctx=ctx)
            qa, qb_, ka, kb_, q1, k1, eq, ek = map(buf, ("qa", "qb_", "ka", "kb_", "q1", "k1", "eq", "ek"))
            phq, phk, vs = map(buf, ("phq", "phk", "vs"))
            U = [buf(f"U{d}") for d in range(D0)]
            S = [buf(f"S{i}") for i in range(2)]
            K = [buf(f"K{m}") for m in range(M0)]
            TT = [[buf(f"T{m}_{d}") for d in range(D0)] for m in range(M0)]
            lden = [buf(f"lden{m}") for m in range(M0)]
            deps = k.sb("deps", [P, 1], ctx=ctx)
            sem = lambda n: ctx.enter_context(nc.semaphore(n))
            (q_mm, k_mm, v_mm, rot, rope_sum, plus1, exped, phi, v_sb, pk_mm, u_done, pq_mm, k_scan, s_scan, t_done,
             kp_done, den_mm, ln_den, rden, coef, sum1, sum2, weighted, y_done, eps_set) = map(sem, (
                 "q_mm", "k_mm", "v_mm", "rot", "rope_sum", "plus1", "exped", "phi", "v_sb", "pk_mm", "u_done", "pq_mm",
                 "k_scan", "s_scan", "t_done", "kp_done", "den_mm", "ln_den", "rden", "coef", "sum1", "sum2", "weighted",
                 "y_done", "deps_set"))
            block = ctx.enter_context(nc.Block())

            @block.tensor
            def _(pe):
                with pe.Fori(0, NCH) as c:
                    h = k.H[:, chunk(c)]
                    pe.wait_ge(u_done, 4 * c + 4)
                    nc.tensor.matmul(ps[2][:], w["wk0"][:], h, start=True, stop=True)
                    nc.tensor.matmul(ps[3][:], w["wk0s"][:], h, start=True, stop=True).then_inc(k_mm, 1)
                    pe.wait_ge(ln_den, 2 * c + 2)
                    nc.tensor.matmul(ps[0][:], w["wq0"][:], h, start=True, stop=True)
                    nc.tensor.matmul(ps[1][:], w["wq0s"][:], h, start=True, stop=True).then_inc(q_mm, 1)
                    pe.wait_ge(t_done, 8 * c + 2)
                    nc.tensor.matmul(ps[4][:], w["wv0"][:], h, start=True, stop=True).then_inc(v_mm, 1)
                    pe.wait_ge(phi, 2 * c + 2)
                    for d in range(D0):
                        nc.tensor.matmul(ps[d][:], w["spread"][:, d, :], phk[:], start=True, stop=True).then_inc(pk_mm, 1)
                    pe.wait_ge(v_sb, c + 1)
                    pe.wait_ge(t_done, 8 * c + 8)
                    for d in range(D0):
                        nc.tensor.matmul(ps[4 + d][:], w["spread"][:, d, :], phq[:], start=True, stop=True).then_inc(pq_mm, 1)
                    for m in range(M0):
                        pe.wait_ge(kp_done, 2 * c + m + 1)
                        pe.wait_ge(u_done, 4 * c + m + 5)
                        nc.tensor.matmul(ps[m][:], w["headsum"][:], K[m][:], start=True, stop=True).then_inc(den_mm, 1)

            @block.scalar
            def _(act):
                act.sem_inc(ln_den, 2)
                nc.scalar.preload_act_table_set(LNEXP)
                act.wait_ge(eps_set, 1)
                with act.Fori(0, NCH) as c:
                    act.wait_ge(rope_sum, 2 * c + 1)
                    nc.scalar.activation(ek[:], ka[:], ACT.Exp).then_inc(exped, 1)
                    nc.scalar.activation(k1[:], ka[:], ACT.Copy, bias=1.0).then_inc(plus1, 1)
                    act.wait_ge(rope_sum, 2 * c + 2)
                    nc.scalar.activation(eq[:], qa[:], ACT.Exp).then_inc(exped, 1)
                    nc.scalar.activation(q1[:], qa[:], ACT.Copy, bias=1.0).then_inc(plus1, 1)
                    act.wait_ge(v_mm, c + 1)
                    act.wait_ge(u_done, 4 * c + 4)
                    nc.scalar.activation(vs[:], ps[4][:], ACT.Copy).then_inc(v_sb, 1)
                    act.wait_ge(y_done, c + 1)
                    for m in range(M0):
                        act.wait_ge(den_mm, 2 * c + m + 1)
                        nc.scalar.activation(lden[m][:], ps[m][:], ACT.Ln, bias=deps[:, 0:1]).then_inc(ln_den, 1)
                        act.wait_ge(ln_den, 2 * c + m + 3)
                        nc.scalar.activation(lden[m][:], lden[m][:], ACT.Exp, scale=-1.0).then_inc(rden, 1)

            @block.vector
            def _(dve):
                nc.vector.memset(deps[:], DEN_EPS).then_inc(eps_set, 1)
                dve.sem_inc(t_done, 8)
                dve.sem_inc(u_done, 4)
                cos, sin = w["rope0"][:, 0, :], w["rope0"][:, 1, :]

                def rotate(c, which):
                    mm, banks, a, b = ((k_mm, (2, 3), ka, kb_), (q_mm, (0, 1), qa, qb_))[which]
                    dve.wait_ge(mm, c + 1)
                    nc.vector.tensor_tensor(a[:], ps[banks[0]][:], cos, ALU.mult)
                    nc.vector.tensor_tensor(b[:], ps[banks[1]][:], sin, ALU.mult).then_inc(rot, 1)

                def features(c, which):
                    e, x1, out = ((ek, k1, phk), (eq, q1, phq))[which]
                    dve.wait_ge(exped, 2 * c + 1 + which)
                    dve.wait_ge(plus1, 2 * c + 1 + which)
                    nc.vector.scalar_tensor_tensor(out[:], e[:], 1.0, x1[:], ALU.min, ALU.max).then_inc(phi, 1)

                def attend(c, more):
                    dve.wait_ge(phi, 2 * c + 1)
                    for m in range(M0):
                        nc.vector.tensor_tensor_scan(K[m][:], beta[m][:, chunk(c)], phk[:], 0.0,
                                                     ALU.mult, ALU.add).then_inc(k_scan, 1)
                    dve.wait_ge(v_sb, c + 1)
                    for d in range(D0):
                        dve.wait_ge(pk_mm, 4 * c + d + 1)
                        nc.vector.tensor_tensor(U[d][:], ps[d][:], vs[:], ALU.mult).then_inc(u_done, 1)
                    for i in range(2 * D0 + 1):
                        if i < 2 * D0:
                            d, m = i // 2, i % 2
                            if m == 0:
                                dve.wait_ge(u_done, 4 * c + d + 5)
                            dve.wait_ge(t_done, 8 * c + i + 7)
                            nc.vector.tensor_tensor_scan(S[i % 2][:], beta[m][:, chunk(c)], U[d][:], 0.0,
                                                         ALU.mult, ALU.add).then_inc(s_scan, 1)
                        if i == 1:
                            dve.wait_ge(y_done, c + 1)
                        if i > 0:
                            d, m = (i - 1) // 2, (i - 1) % 2
                            if m == 0:
                                dve.wait_ge(pq_mm, 4 * c + d + 1)
                            dve.wait_ge(s_scan, 8 * c + i)
                            nc.vector.tensor_tensor(TT[m][d][:], ps[4 + d][:], S[(i - 1) % 2][:],
                                                    ALU.mult).then_inc(t_done, 1)
                        if more and i in (3, 4):
                            rotate(c + 1, i - 3)
                        if more and i in (6, 8):
                            if i == 6:
                                dve.wait_ge(den_mm, 2 * c + 2)
                            features(c + 1, (i - 6) // 2)

                rotate(0, 0)
                rotate(0, 1)
                features(0, 0)
                features(0, 1)
                with dve.Fori(0, NCH - 1) as c:
                    attend(c, True)
                attend(NCH - 1, False)

            @block.gpsimd
            def _(pool):
                pool.sem_inc(y_done, 1)

                def rope(c):
                    for i, (a, b) in enumerate(((ka, kb_), (qa, qb_))):
                        wait_alone(k, pool, rot, 2 * c + i + 1)
                        nc.gpsimd.tensor_tensor(a[:], a[:], b[:], ALU.add).then_inc(rope_sum, 1)

                def combine(c, more):
                    wait_alone(k, pool, phi, 2 * c + 2)
                    for m in range(M0):
                        wait_alone(k, pool, k_scan, 2 * c + m + 1)
                        nc.gpsimd.tensor_tensor(K[m][:], K[m][:], phq[:], ALU.mult).then_inc(kp_done, 1)
                    for m in range(M0):
                        wait_alone(k, pool, rden, 2 * c + m + 1)
                        nc.gpsimd.tensor_tensor(lden[m][:], lden[m][:], mix[m][:, chunk(c)], ALU.mult).then_inc(coef, 1)
                    for d in (0, 2):
                        for m in range(M0):
                            wait_alone(k, pool, t_done, 8 * c + 2 * (d + 1) + m + 9)
                            nc.gpsimd.tensor_tensor(TT[m][d][:], TT[m][d][:], TT[m][d + 1][:],
                                                    ALU.add).then_inc(sum1, 1)
                        if more and d == 0:
                            rope(c + 1)
                    for m in range(M0):
                        wait_alone(k, pool, sum1, 4 * c + m + 3)
                        nc.gpsimd.tensor_tensor(TT[m][0][:], TT[m][0][:], TT[m][2][:], ALU.add).then_inc(sum2, 1)
                    for m in range(M0):
                        wait_alone(k, pool, sum2, 2 * c + m + 1)
                        wait_alone(k, pool, coef, 2 * c + m + 1)
                        nc.gpsimd.tensor_tensor(TT[m][0][:], TT[m][0][:], lden[m][:], ALU.mult).then_inc(weighted, 1)
                    wait_alone(k, pool, weighted, 2 * c + 2)
                    nc.gpsimd.tensor_tensor(Y[:, chunk(c)], TT[0][0][:], TT[1][0][:], ALU.add).then_inc(y_done, 1)

                rope(0)
                with pool.Fori(0, NCH - 1) as c:
                    combine(c, True)
                combine(NCH - 1, False)

        with ExitStack() as ctx:
            W = 2
            z = [k.sb(f"z{i}", [P, CH], ctx=ctx) for i in range(W)]
            zn = [k.sb(f"zn{i}", [P, CH], ctx=ctx) for i in range(W)]
            b1 = [ln_buffers(k, ctx, f"nz{i}", 4 * i + 1, 4 * i + 2) for i in range(W)]
            b2 = [ln_buffers(k, ctx, f"nx{i}", 4 * i + 3, 4 * i + 2) for i in range(W)]
            s1, s2 = ln_sems(nc, ctx, "nz"), ln_sems(nc, ctx, "nx")
            sem = lambda n: ctx.enter_context(nc.semaphore(n))
            o_mm, z_done, affine, resid = map(sem, ("o_mm", "z_done", "affine0", "resid0"))
            block = ctx.enter_context(nc.Block())

            @block.tensor
            def _(pe):
                with pe.Fori(0, NCH // W) as c2:
                    for i in range(W):
                        c = W * c2 + i
                        pe.wait_ge(z_done, c + 1)
                        nc.tensor.matmul(ps[4 * i][:], w["wout0"][:], Y[:, chunk(c)], start=True, stop=True).then_inc(o_mm, 1)
                    for i in range(W):
                        c = W * c2 + i
                        pe.wait_ge(z_done, c + 1 + W)
                        ln_centre(k, pe, s1, b1[i], c + 1, z[i][:])
                    for i in range(W):
                        pe.wait_ge(s2.rstd, W * c2 + i + 1)
                        ln_variance(k, pe, s1, b1[i], W * c2 + i + 1)
                    for i in range(W):
                        c = W * c2 + i
                        pe.wait_ge(resid, c + 1)
                        ln_centre(k, pe, s2, b2[i], c + 1, k.XT[:, chunk(c)])
                    for i in range(W):
                        ln_variance(k, pe, s2, b2[i], W * c2 + i + 1)

            @block.scalar
            def _(act):
                nc.scalar.preload_act_table_set(LNEXP)
                act.sem_inc(s2.rstd, W)
                with act.Fori(0, NCH // W) as c2:
                    for i in range(W):
                        ln_square(k, act, s1, b1[i], W * c2 + i + 1)
                    for i in range(W):
                        ln_rstd(k, act, s1, b1[i], W * c2 + i + 1)
                    for i in range(W):
                        ln_square(k, act, s2, b2[i], W * c2 + i + 1)
                    for i in range(W):
                        ln_rstd(k, act, s2, b2[i], W * c2 + i + 1)

            @block.vector
            def _(dve):
                dve.sem_inc(s1.normed, W)
                dve.sem_inc(s2.normed, W)
                dve.sem_inc(z_done, W)
                with dve.Fori(0, NCH // W) as c2:
                    for i in range(W):
                        c = W * c2 + i
                        dve.wait_ge(o_mm, c + 1)
                        nc.vector.scalar_tensor_tensor(z[i][:], ps[4 * i][:], w["vec0"][:, 4:5], k.H[:, chunk(c)],
                                                       ALU.add, ALU.add).then_inc(z_done, 1)
                    for i in range(W):
                        c = W * c2 + i
                        ln_scale(k, dve, s1, b1[i], c + 1, zn[i][:])
                        dve.wait_ge(s1.normed, c + 1 + W)
                        nc.vector.tensor_scalar(zn[i][:], zn[i][:], w["vec0"][:, 5:6], w["vec0"][:, 6:7],
                                                ALU.mult, ALU.add).then_inc(affine, 1)
                        dve.wait_ge(affine, c + 1)
                        nc.vector.tensor_tensor(k.XT[:, chunk(c)], k.XT[:, chunk(c)], zn[i][:], ALU.add).then_inc(resid, 1)
                    for i in range(W):
                        c = W * c2 + i
                        dve.wait_ge(s2.rstd, c + 1 + W)
                        ln_scale(k, dve, s2, b2[i], c + 1, k.H[:, chunk(c)])


def experts(k):
    nc, ps = k.nc, k.ps
    with ExitStack() as big:
        small = ["b1e", "b2e", "pick"]
        large = ["w1e", "w2e"]
        w = {n: k.const[n] for n in ROUTING}
        for n in small:
            w[n] = k.sb(n, list(k.dram[n].shape), k.dram[n].dtype, big)
        wide = {n: [k.sb(f"{n}_{part}", [P, NX, FFI], F32R, big) for part in ("hi", "lo")] for n in large}
        wT = k.sb("wT", [P, T], BF16, big)
        with ExitStack() as ctx:
            raw = {n: k.sb(f"{n}_raw", list(k.dram[n].shape), F32, ctx) for n in large}
            s3 = lambda n, e=NE, d=F32: k.sb(n, [P, NT, e], d, ctx)
            pr, oh1, oh2, val, eq, Wt = (s3(n) for n in ("probs", "oh1", "oh2", "val", "eqm", "Wt"))
            W9, R9 = s3("W9", NX), s3("R9", NX)
            parts = s3("parts", NPART * NX, BF16)
            cols = k.sb("cols", [P, 14, NT], F32, ctx)
            mx, sm, rs_, p1, v1, p2, v2, w1, w2, fb, pos, inc, over, one = (cols[:, i, :] for i in range(14))
            elig = k.sb("elig", [P, NT], BF16, ctx)
            eligf = k.sb("eligf", [P, NT], F32, ctx)
            sem = lambda n: ctx.enter_context(nc.semaphore(n))
            wT_zero, logit_mm, shifted, exped, step, elig_r, counted, parts_r, turned, turned_sb = map(sem, (
                "wT_zero", "logit_mm", "shifted", "exped_r", "dve_step", "elig_r", "counted", "parts_r", "turned",
                "turned_sb"))
            large_in, w_hi, w_lo = sem("large_in"), k.w_hi, k.w_lo
            block = ctx.enter_context(nc.Block())
            bc = lambda a: a.rearrange("p (n o) -> p n o", o=1).to_broadcast([P, NT, NE])
            flat = lambda t, e: t[:, e, :] if len(t.shape) == 3 else t[:, e, :, :].rearrange("p a b -> p (a b)")

            @block.sync
            def _(sp):
                for n in large:
                    sp.dma_start(raw[n][:], k.dram[n]).then_inc(large_in, 16)
                for n in small:
                    sp.dma_start(w[n][:], k.dram[n]).then_inc(large_in, 16)
                sp.wait_ge(large_in, 16 * 5)

            @block.tensor
            def _(pe):
                pe.wait_ge(k.late_in, 16 * N_LATE)
                for n in range(NT):
                    i = nc.tensor.matmul(ps[0][:, n * NE:(n + 1) * NE], k.H[:, n * P:(n + 1) * P], w["wr"][:],
                                         start=True, stop=True)
                i.then_inc(logit_mm, 1)
                for e in range(NE):
                    pe.wait_ge(elig_r, e + 1)
                    nc.tensor.matmul(ps[1][:, 0:NT], w["tri"][:], elig[:], start=True, stop=True)
                    nc.tensor.matmul(ps[2][:, 0:NT], w["ones"][:], elig[:], start=True, stop=True).then_inc(counted, 1)
                pe.wait_ge(parts_r, 1)
                for n in range(NT):
                    bank = ps[3 + n // 8][:].bitcast(BF16)
                    i = nc.tensor.transpose(bank[0:NPART * NX, (n % 8) * P:(n % 8 + 1) * P], parts[:, n, :], k.const["identb"][:])
                    if n % 8 == 7:
                        i.then_inc(turned, 1)

            @block.gpsimd
            def _(pool):
                nc.gpsimd.memset(wT[:], 0.0).then_inc(wT_zero, 1)
                for q, n in enumerate(large):
                    for e in range(NX):
                        pool.wait_ge(w_hi, q * NX + e + 1)
                        nc.gpsimd.tensor_tensor(wide[n][1][:, e, :], flat(raw[n], e), wide[n][0][:, e, :].bitcast(F32),
                                                ALU.subtract).then_inc(w_lo, 1)
                pool.wait_ge(w_lo, 2 * NX)

            @block.scalar
            def _(act):
                act.wait_ge(shifted, 1)
                nc.scalar.activation(pr[:], pr[:], ACT.Exp).then_inc(exped, 1)
                act.wait_ge(large_in, 16 * 5)
                for n in large:
                    for e in range(NX):
                        nc.scalar.activation(wide[n][0][:, e, :], flat(raw[n], e), ACT.Copy).then_inc(w_hi, 1)
                act.wait_ge(wT_zero, 1)
                for q in range(NT // 8):
                    act.wait_ge(turned, q + 1)
                    nc.scalar.activation(wT[0:NPART * NX, q * 8 * P:(q + 1) * 8 * P], ps[3 + q][:].bitcast(BF16)[0:NPART * NX, :],
                                         ACT.Copy).then_inc(turned_sb, 1)
                act.wait_ge(turned_sb, NT // 8)

            @block.vector
            def _(dve):
                V = nc.vector
                done = [0]

                def after(ins):
                    done[0] += 1
                    ins.then_inc(step, 1)
                    dve.wait_ge(step, done[0])

                dve.wait_ge(k.late_in, 16 * N_LATE)
                dve.wait_ge(logit_mm, 1)
                lg = ps[0][:, 0:NT * NE].rearrange("p (n e) -> p n e", e=NE)
                after(V.tensor_reduce(mx, lg, AX.X, ALU.max))
                V.tensor_tensor(pr[:], lg, bc(mx), ALU.subtract).then_inc(shifted, 1)
                dve.wait_ge(exped, 1)
                after(V.tensor_reduce(sm, pr[:], AX.X, ALU.add))
                after(V.reciprocal(rs_, sm))
                after(V.tensor_tensor(pr[:], pr[:], bc(rs_), ALU.mult))
                for p_, v_, oh in ((p1, v1, oh1), (p2, v2, oh2)):
                    after(V.tensor_reduce(p_, pr[:], AX.X, ALU.max))
                    after(V.tensor_tensor(eq[:], pr[:], bc(p_), ALU.is_equal))
                    after(V.tensor_tensor(val[:], eq[:], w["iota8"][:], ALU.mult))
                    after(V.tensor_reduce(v_, val[:], AX.X, ALU.min))
                    after(V.tensor_tensor(oh[:], w["iota8"][:], bc(v_), ALU.is_equal))
                    if oh is oh1:
                        after(V.scalar_tensor_tensor(pr[:], oh1[:], -2.0, pr[:], ALU.mult, ALU.add))
                after(V.tensor_tensor(sm, p1, p2, ALU.add))
                after(V.tensor_scalar(sm, sm, 1e-9, None, ALU.max))
                after(V.reciprocal(rs_, sm))
                after(V.tensor_tensor(w1, p1, rs_, ALU.mult))
                after(V.tensor_tensor(w2, p2, rs_, ALU.mult))
                after(V.tensor_tensor(Wt[:], oh1[:], bc(w1), ALU.mult))
                after(V.tensor_tensor(val[:], oh2[:], bc(w2), ALU.mult))
                after(V.tensor_tensor(Wt[:], Wt[:], val[:], ALU.add))
                after(V.tensor_tensor(oh1[:], oh1[:], oh2[:], ALU.add))
                after(V.memset(fb, 0.0))
                after(V.memset(one, 1.0))
                for e in range(NE):
                    after(V.tensor_tensor(eligf[:], oh1[:, :, e], fb, ALU.is_gt))
                    V.tensor_copy(elig[:], eligf[:]).then_inc(elig_r, 1)
                    dve.wait_ge(counted, e + 1)
                    after(V.tensor_tensor_scan(inc, one, ps[2][:, 0:NT], 0.0, ALU.mult, ALU.add))
                    after(V.tensor_tensor(inc, inc, ps[2][:, 0:NT], ALU.subtract))
                    after(V.tensor_tensor(pos, inc, ps[1][:, 0:NT], ALU.add))
                    after(V.scalar_tensor_tensor(over, pos, float(CAP), eligf[:], ALU.is_gt, ALU.mult))
                    after(V.tensor_tensor(fb, fb, over, ALU.max))
                after(V.tensor_tensor(over, one, fb, ALU.subtract))
                after(V.tensor_tensor(W9[:, :, 0:NE], Wt[:], bc(over), ALU.mult))
                after(V.tensor_copy(W9[:, :, NE], fb))
                after(V.tensor_copy(parts[:, :, 0:NX], W9[:]))
                after(V.tensor_tensor(R9[:], W9[:], parts[:, :, 0:NX], ALU.subtract))
                after(V.tensor_copy(parts[:, :, NX:2 * NX], R9[:]))
                after(V.tensor_tensor(R9[:], R9[:], parts[:, :, NX:2 * NX], ALU.subtract))
                after(V.tensor_copy(parts[:, :, 2 * NX:3 * NX], R9[:]))
                dve.sem_inc(parts_r, 1)

        with ExitStack() as ctx:
            G = k.sb("G", [P, NJ, CH], ctx=ctx)
            Gp = [k.sb(f"G_{part}", [P, 3, NJ, CH], F32R, ctx) for part in ("hi", "lo")]
            Hp = [k.sb(f"H_{part}", [P, 2, CH], F32R, ctx) for part in ("hi", "lo")]
            WE = k.sb("WE", [P, 3, CH], ctx=ctx)
            Z = k.sb("Z", [P, 3, CH], ctx=ctx)
            acc = k.sb("acc", [P, CH], ctx=ctx)
            sem = lambda n: ctx.enter_context(nc.semaphore(n))
            h_parts, h_mm, gelu, g_parts, y_mm, spread_mm, spread_sb, z_done, added, resid = map(sem, (
                "h_parts", "h_mm", "gelu", "g_parts", "ye_mm", "spread_mm", "spread_sb", "ze_done", "added",
                "resid_e"))
            block = ctx.enter_context(nc.Block())

            @block.tensor
            def _(pe):
                pe.sem_inc(y_mm, 3)

                def step(c, par):
                    for i in range(NX + 1):
                        if i == 0:
                            pe.wait_ge(h_parts, 2 * c + 2)
                        if i < NX:
                            for j in range(NJ):
                                pe.wait_ge(gelu, (c * NX + i) * NJ + j + 1)
                                for a, b in PASSES:
                                    o = nc.tensor.matmul(ps[j][:], wide["w1e"][a][:, i, j * P:(j + 1) * P], Hp[b][:, par, :],
                                                         start=(a + b == 0), stop=(a == 1))
                                o.then_inc(h_mm, 1)
                        if i > 0:
                            e = i - 1
                            wait_alone(k, pe, spread_sb, c * NX + e + 1)
                            nc.tensor.matmul(ps[7][:], w["pick"][:, e * P:(e + 1) * P], wT[:, chunk(c)],
                                             start=True, stop=True).then_inc(spread_mm, 1)
                            pe.wait_ge(z_done, c * NX + e + 1)
                            for j in range(NJ):
                                pe.wait_ge(g_parts, 2 * ((c * NX + e) * NJ + NJ + j + 1))
                                for a, b in PASSES:
                                    o = nc.tensor.matmul(ps[4 + e % 3][:], wide["w2e"][a][:, e, j * P:(j + 1) * P],
                                                         Gp[b][:, e % 3, j, :], start=(j == 0 and a + b == 0),
                                                         stop=(j == NJ - 1 and a == 1))
                            o.then_inc(y_mm, 1)

                with pe.Fori(0, NCH // 2) as x:
                    step(2 * x, 0)
                    step(2 * x + 1, 1)

            @block.scalar
            def _(act):
                act.sem_inc(gelu, NJ)
                act.sem_inc(spread_sb, 1)
                nc.scalar.preload_act_table(ACT.Gelu)
                with act.Fori(0, NCH) as c:
                    for i in range(NX + 1):
                        if i < NX:
                            for j in range(NJ):
                                n = (c * NX + i) * NJ + j
                                act.wait_ge(h_mm, n + 1)
                                act.wait_ge(g_parts, 2 * n + 2)
                                nc.scalar.activation(G[:, j, :], ps[j][:], ACT.Gelu,
                                                     bias=w["b1e"][:, i, j:j + 1]).then_inc(gelu, 1)
                        if i > 0:
                            e = i - 1
                            act.wait_ge(spread_mm, c * NX + e + 1)
                            act.wait_ge(z_done, c * NX + e + 1)
                            nc.scalar.activation(WE[:, e % 3, :], ps[7][:], ACT.Copy).then_inc(spread_sb, 1)

            @block.vector
            def _(dve):
                V = nc.vector
                dve.sem_inc(z_done, 3)
                dve.sem_inc(resid, 1)
                dve.sem_inc(g_parts, 2 * NJ)

                def split_input(c, par):
                    V.tensor_scalar(Hp[0][:, par, :], k.H[:, chunk(c)], 1.0, None, ALU.mult).then_inc(h_parts, 1)
                    dve.wait_ge(h_parts, 2 * c + 1)
                    V.tensor_tensor(Hp[1][:, par, :], k.H[:, chunk(c)], Hp[0][:, par, :].bitcast(F32), ALU.subtract).then_inc(h_parts, 1)

                def split_gelu(c, i, j):
                    n = (c * NX + i) * NJ + j
                    dve.wait_ge(gelu, n + NJ + 1)
                    if j == 0:
                        dve.wait_ge(y_mm, c * NX + i + 1)
                    V.tensor_scalar(Gp[0][:, i % 3, j, :], G[:, j, :], 1.0, None, ALU.mult).then_inc(g_parts, 1)
                    dve.wait_ge(g_parts, 2 * (n + NJ) + 1)
                    V.tensor_tensor(Gp[1][:, i % 3, j, :], G[:, j, :], Gp[0][:, i % 3, j, :].bitcast(F32),
                                    ALU.subtract).then_inc(g_parts, 1)

                def step(c, par):
                    for i in range(NX + 1):
                        if i < NX:
                            for j in range(NJ):
                                split_gelu(c, i, j)
                        if i == NX // 2:
                            dve.wait_ge(gelu, c * NX * NJ + NJ)
                            split_input(c + 1, 1 - par)
                        if i > 0:
                            e = i - 1
                            dve.wait_ge(y_mm, c * NX + e + 4)
                            dve.wait_ge(spread_sb, c * NX + e + 2)
                            dve.wait_ge(added, c * NX + e + 1)
                            V.scalar_tensor_tensor(Z[:, e % 3, :], ps[4 + e % 3][:], w["b2e"][:, e:e + 1],
                                                   WE[:, e % 3, :], ALU.add, ALU.mult).then_inc(z_done, 1)
                    dve.wait_ge(added, (c + 1) * NX + 3)
                    V.tensor_tensor(k.XT[:, chunk(c)], k.XT[:, chunk(c)], acc[:], ALU.add).then_inc(resid, 1)

                split_input(0, 0)
                with dve.Fori(0, NCH // 2) as x:
                    step(2 * x, 0)
                    step(2 * x + 1, 1)

            @block.gpsimd
            def _(pool):
                pool.sem_inc(added, 3)
                with pool.Fori(0, NCH) as c:
                    for e in range(1, NX):
                        wait_alone(k, pool, z_done, c * NX + e + 4)
                        if e == 1:
                            wait_alone(k, pool, resid, c + 1)
                            nc.gpsimd.tensor_tensor(acc[:], Z[:, 0, :], Z[:, 1, :], ALU.add).then_inc(added, 2)
                        else:
                            wait_alone(k, pool, added, c * NX + e + 3)
                            nc.gpsimd.tensor_tensor(acc[:], acc[:], Z[:, e % 3, :], ALU.add).then_inc(added, 1)


SPLIT = ("wqkv", "wqks")
V_LG, V_LB, V_B2, V_B1A, V_B1G, V_QS, V_KS, V_QSS, V_KSS = 0, 1, 2, 3, 6, 9, 10, 11, 12


def layer_buffers(k, shared):
    k.lw = {n: [k.sb(f"{n}_{part}", list(k.dram[n].shape)[1:], F32R) for part in ("hi", "lo")] for n in SPLIT}
    k.tab = k.sb("tab", [P, 4, CH])
    k.sel = k.sb("sel", [P, NU, P], BF16)
    k.vec2 = [k.sb(f"vec2_{l}", list(k.dram["vec2"].shape)[1:]) for l in range(DEPTH)]
    k.raw_in, k.prepared = map(shared, ("raw_in", "prepared"))


def raw_buffers(k, l, ctx):
    return {n: k.sb(f"{n}_raw{l}", list(k.dram[n].shape)[-2:] if n in SPLIT else list(k.dram[n].shape), ctx=ctx)
            for n in (*SPLIT, "xpos")}


def prepare_loads(k, l, raw, sp):
    for n in SPLIT:
        sp.dma_start(raw[n][:], k.dram[n][l]).then_inc(k.raw_in, 16)
    sp.dma_start(raw["xpos"][:], k.dram["xpos"]).then_inc(k.raw_in, 16)
    sp.dma_start(k.vec2[l][:], k.dram["vec2"][l]).then_inc(k.raw_in, 16)
    if l == 0:
        sp.dma_start(k.sel[:], k.dram["rowsel"]).then_inc(k.raw_in, 16)


def prepare_split(k, l, raw, pool):
    nc = k.nc
    pool.wait_ge(k.raw_in, 16 * (4 * l + 5))
    n = sum(k.dram[name].shape[-1] for name in SPLIT) // CH * l + 2 * NX
    for name in SPLIT:
        for q in range(k.dram[name].shape[-1] // CH):
            hi, lo = (t[:, q * CH:(q + 1) * CH] for t in k.lw[name])
            src = raw[name][:, q * CH:(q + 1) * CH]
            nc.gpsimd.tensor_scalar(hi, src, 1.0, None, ALU.mult).then_inc(k.w_hi, 1)
            n += 1
            pool.wait_ge(k.w_hi, n)
            nc.gpsimd.tensor_tensor(lo, src, hi.bitcast(F32), ALU.subtract).then_inc(k.w_lo, 1)
    for i, c in enumerate((V_QS, V_QSS, V_KS, V_KSS)):
        nc.gpsimd.tensor_scalar(k.tab[:, i, :], raw["xpos"][:, i, :], k.vec2[l][:, c:c + 1], None,
                                ALU.mult).then_inc(k.prepared, 1)
    pool.wait_ge(k.w_lo, n)
    pool.wait_ge(k.prepared, 4 * (l + 1))


def retention(k):
    nc, ps = k.nc, k.ps
    with ExitStack() as big:
        w = {n: k.const[n] for n in RETENTION}
        G = k.sb("G1", [P, T], ctx=big)
        Y = k.sb("Y1", [P, T], ctx=big)
        with ExitStack() as ctx:
            W = 2
            raw = raw_buffers(k, 0, ctx)
            dec = k.sb("dec", [P, CH], ctx=ctx)
            h, st, y, yn = ([k.sb(f"{n}{i}", [P, CH], ctx=ctx) for i in range(W)] for n in ("h1", "st1", "y1", "yn1"))
            b1 = [ln_buffers(k, ctx, f"na{i}", 4 * i, 4 * i + 1) for i in range(W)]
            b2 = [ln_buffers(k, ctx, f"nb{i}", 4 * i + 1, 4 * i + 2) for i in range(W)]
            s1, s2 = ln_sems(nc, ctx, "na"), ln_sems(nc, ctx, "nb")
            sem = lambda n: ctx.enter_context(nc.semaphore(n))
            dec_r, v_mm, q_mm, g_mm, g_sb, state, y_r, aff = map(sem, (
                "dec_r", "v1_mm", "q1_mm", "g1_mm", "g1_sb", "state1", "y1_r", "affine1"))
            block = ctx.enter_context(nc.Block())

            @block.sync
            def _(sp):
                prepare_loads(k, 0, raw, sp)

            @block.gpsimd
            def _(pool):
                prepare_split(k, 0, raw, pool)

            @block.tensor
            def _(pe):
                pe.wait_ge(k.late_in, 16 * N_LATE)
                with pe.Fori(0, NCH // W) as c2:
                    for i in range(W):
                        pe.wait_ge(g_sb, W * c2 + i + 1)
                        ln_centre(k, pe, s1, b1[i], W * c2 + i + 1, k.XT[:, chunk(W * c2 + i)])
                    for i in range(W):
                        pe.wait_ge(s2.normed, W * c2 + i + 1)
                        ln_variance(k, pe, s1, b1[i], W * c2 + i + 1)
                    for i in range(W):
                        c = W * c2 + i
                        pe.wait_ge(s1.normed, c + 1 + W)
                        pe.wait_ge(y_r, c + 1)
                        nc.tensor.matmul(ps[4 * i + 3][:], w["wv1"][:], h[i][:], start=True, stop=True).then_inc(v_mm, 1)
                        nc.tensor.matmul(ps[4 * i + 2][:], w["wq1"][:], h[i][:], start=True, stop=True).then_inc(q_mm, 1)
                        nc.tensor.matmul(ps[4 * i][:], w["wg1"][:], h[i][:], start=True, stop=True).then_inc(g_mm, 1)
                    for i in range(W):
                        pe.wait_ge(y_r, W * c2 + i + 1 + W)
                        ln_centre(k, pe, s2, b2[i], W * c2 + i + 1, y[i][:])
                    for i in range(W):
                        ln_variance(k, pe, s2, b2[i], W * c2 + i + 1)

            @block.scalar
            def _(act):
                act.sem_inc(g_sb, W)
                nc.scalar.preload_act_table_set(LNEXP)
                with act.Fori(0, NCH // W) as c2:
                    for i in range(W):
                        ln_square(k, act, s1, b1[i], W * c2 + i + 1)
                    for i in range(W):
                        ln_rstd(k, act, s1, b1[i], W * c2 + i + 1)
                    for i in range(W):
                        act.wait_ge(g_mm, W * c2 + i + 1)
                        nc.scalar.activation(G[:, chunk(W * c2 + i)], ps[4 * i][:], ACT.Copy).then_inc(g_sb, 1)
                    for i in range(W):
                        ln_square(k, act, s2, b2[i], W * c2 + i + 1)
                    for i in range(W):
                        ln_rstd(k, act, s2, b2[i], W * c2 + i + 1)

            @block.vector
            def _(dve):
                dve.sem_inc(s1.normed, W)
                dve.sem_inc(s2.normed, W)
                dve.sem_inc(y_r, W)
                dve.wait_ge(k.late_in, 16 * N_LATE)
                nc.vector.tensor_copy(dec[:], w["vec1"][:, 0:1].to_broadcast([P, CH])).then_inc(dec_r, 1)
                dve.wait_ge(dec_r, 1)
                nc.vector.memset(dec[:].rearrange("p (s t) -> p s t", t=SEQ)[:, :, 0:1], 0.0).then_inc(dec_r, 1)
                dve.wait_ge(dec_r, 2)
                with dve.Fori(0, NCH // W) as c2:
                    for i in range(W):
                        ln_scale(k, dve, s1, b1[i], W * c2 + i + 1, h[i][:])
                    for i in range(W):
                        c = W * c2 + i
                        dve.wait_ge(v_mm, c + 1)
                        nc.vector.tensor_tensor_scan(st[i][:], dec[:], ps[4 * i + 3][:], 0.0,
                                                     ALU.mult, ALU.add).then_inc(state, 1)
                        dve.wait_ge(q_mm, c + 1)
                        dve.wait_ge(state, c + 1)
                        nc.vector.tensor_tensor(y[i][:], ps[4 * i + 2][:], st[i][:], ALU.mult).then_inc(y_r, 1)
                    for i in range(W):
                        c = W * c2 + i
                        ln_scale(k, dve, s2, b2[i], c + 1, yn[i][:])
                        dve.wait_ge(s2.normed, c + 1 + W)
                        nc.vector.tensor_scalar(Y[:, chunk(c)], yn[i][:], w["vec1"][:, 1:2], w["vec1"][:, 2:3],
                                                ALU.mult, ALU.add).then_inc(aff, 1)
                    dve.wait_ge(g_mm, W * c2 + W)
                    dve.wait_ge(aff, W * c2 + W)

        with ExitStack() as ctx:
            sg = k.sb("sg", [P, 2, CH], ctx=ctx)
            sem = lambda n: ctx.enter_context(nc.semaphore(n))
            silu, gated, o_mm, resid = map(sem, ("silu", "gated", "o1_mm", "resid1"))
            block = ctx.enter_context(nc.Block())

            @block.scalar
            def _(act):
                with act.Fori(0, NCH) as c:
                    nc.scalar.activation(G[:, chunk(c)], G[:, chunk(c)], ACT.Silu).then_inc(silu, 1)

            @block.gpsimd
            def _(pool):
                with pool.Fori(0, NCH) as c:
                    wait_alone(k, pool, silu, c + 1)
                    nc.gpsimd.tensor_tensor(Y[:, chunk(c)], Y[:, chunk(c)], G[:, chunk(c)], ALU.mult).then_inc(gated, 1)

            @block.tensor
            def _(pe):
                with pe.Fori(0, NCH // 2) as c2:
                    for i in range(2):
                        pe.wait_ge(gated, 2 * c2 + i + 1)
                        pe.wait_ge(resid, 2 * c2 + i + 1)
                        nc.tensor.matmul(ps[i][:], w["wo1"][:], Y[:, chunk(2 * c2 + i)], start=True, stop=True).then_inc(o_mm, 1)

            @block.vector
            def _(dve):
                dve.sem_inc(resid, 2)
                with dve.Fori(0, NCH // 2) as c2:
                    for i in range(2):
                        dve.wait_ge(o_mm, 2 * c2 + i + 1)
                        cc = chunk(2 * c2 + i)
                        nc.vector.tensor_tensor(k.XT[:, cc], ps[i][:], k.XT[:, cc], ALU.add).then_inc(resid, 1)


def later(a):
    return a.rearrange("p (s t) -> p s t", t=SEQ)[:, :, 1:SEQ]


def shifted_views(k, cols):
    return k.H[0:DH, cols], k.H[DH:P, cols].rearrange("p (s t) -> p s t", t=SEQ)[:, :, 0:SEQ - 1]


def shift_tokens(k, done, dst, cols):
    first, last = shifted_views(k, cols)
    k.nc.vector.tensor_copy(dst[0:DH, :], first)
    k.nc.vector.tensor_copy(later(dst[DH:P, :]), last).then_inc(done, 1)


NU = HEADS * SPC
HALF = NU // 2
EARLY = 3
LATE = EARLY + HALF // 2
KW = P + WIN


def need(eng, sem, value):
    if not isinstance(value, int) or value > 0:
        eng.wait_ge(sem, value)


def local_layer(k, l, shared):
    here = lambda g: chunk(g - l * NCH)
    G0, G1, L = l * NCH, (l + 1) * NCH, l + 1
    nc, ps = k.nc, k.ps
    NBLK = 2 * NB
    with ExitStack() as big:
        names = ["wo2", "w1f", "w2f"]
        w = {"vec2": k.vec2[l]}
        for n in names:
            w[n] = k.sb(f"{n}_{l}", list(k.dram[n].shape)[1:], F32, big)
        with ExitStack() as ctx:
            two = lambda n, rows=P: k.sb(f"{n}{l}", [rows, 2, CH], ctx=ctx)
            tab, sel = k.tab, k.sel
            hs = [[k.sb(f"hs{l}_{part}{i}", [P, CH], F32R, ctx) for i in range(2)] for part in ("hi", "lo")]
            sq, cl, rn, ra, rb = (two(n) for n in ("sqb", "cl", "rn", "ra", "rb"))
            QK = [k.sb(f"QK{l}_{i}", [P, NBLK, CH], ctx=ctx) for i in range(2)]
            QKr = k.sb(f"QKr{l}", [P, NBLK, CH], F32R, ctx)
            VA = [k.sb(f"VA{l}_{i}", [P, CH // P, HEADS, 2 * DH], ctx=ctx) for i in range(2)]
            PT = k.sb(f"PT{l}", [P, 2, KW + P], ctx=ctx)
            OT = k.sb(f"OT{l}", [P, NB, CH], ctx=ctx)
            rd = two("rd", DH)
            nm = k.sb(f"nm{l}", [P, 2 * NU], ctx=ctx)
            hl = [k.sb(f"hl{l}_{i}", [P, P], BF16, ctx) for i in range(2)]
            mT = [k.sb(f"mT{l}_{i}", [P, P], BF16, ctx) for i in range(2)]
            lnb = k.sb(f"lnb{l}", [P, 1], ctx=ctx)
            (w_in, made, hs_hi, zeroed, shifted, proj, v_mm, v_sb, squared, ssq, clipped, logged, rnorm, rotated,
             summed, qk_r, qkr_r, s_mm, max_r, hi_r, hl_r, mT_mm, mT_r, st_mm, pt_r, av_mm, ld_r, rd_r, o_r, x_mm,
             resid) = map(shared, (
                 "w_in", "made", "hs_hi", "zeroed", "shifted", "proj", "v_mm", "v_sb", "squared", "ssq", "clipped",
                 "logged", "rnorm", "rotated", "summed", "qk_r", "qkr_r", "s_mm", "max_r", "hi_r", "hl_r", "mT_mm",
                 "mT_r", "st_mm", "pt_r", "av_mm", "ld_r", "rd_r", "o_r", "x_mm", "resid"))
            BA, BB, BS, BM, BT, BO = 0, 1, 2, 3, 4, 6
            col = lambda blk: blk // 2 + NB * (blk % 2)
            where = lambda u: (u // SPC, u % SPC, DH * (u // SPC % 2), u // SPC // 2, u % SPC * SEQ)
            block = ctx.enter_context(nc.Block())

            def steps(eng, step):
                step(G0, 0, True, False, False)
                step(G0 + 1, 1, True, True, False)
                with eng.Fori(0, NCH // 2 - 1) as x:
                    step(2 * x + (G0 + 2), 0, True, True, True)
                    step(2 * x + (G0 + 3), 1, True, True, True)
                step(G0 + NCH, 0, False, True, True)

            @block.sync
            def _(sp):
                for n in names:
                    sp.dma_start(w[n][:], k.dram[n][l]).then_inc(w_in, 16)

            @block.gpsimd
            def _(pool):
                for i in range(2):
                    nc.gpsimd.memset(hl[i][:], 0.0).then_inc(zeroed, 1)
                for i in range(2):
                    nc.gpsimd.memset(VA[i][:], 1.0).then_inc(zeroed, 1)
                pool.wait_ge(zeroed, 4 * L)

                def step(g, par, project, attend, finish):
                    if project:
                        for blk in range(NBLK):
                            n = NBLK * g + blk
                            wait_alone(k, pool, rotated, n + 1)
                            nc.gpsimd.tensor_tensor(ra[:, blk % 2, :], ra[:, blk % 2, :], rb[:, blk % 2, :],
                                                    ALU.add).then_inc(summed, 1)
                            if blk == 0 and (not isinstance(g, int) or g > 1):
                                wait_alone(k, pool, st_mm, NU * (g - 1))
                            wait_alone(k, pool, summed, n + 1)
                            wait_alone(k, pool, rnorm, n + 1)
                            nc.gpsimd.tensor_tensor(QK[par][:, col(blk), :], ra[:, blk % 2, :], rn[:, blk % 2, :],
                                                    ALU.mult).then_inc(qk_r, 1)

                steps(pool, step)

            @block.tensor
            def _(pe):
                pe.wait_ge(zeroed, 4 * L)

                def project_block(g, par, blk):
                    n = NBLK * g + blk
                    if blk == 0:
                        pe.wait_ge(shifted, g + 1 + l)
                    need(pe, rotated, n)
                    i = col(blk)
                    for bank, name in ((BA, "wqkv"), (BB, "wqks")):
                        for wp, hp in PASSES:
                            m = nc.tensor.matmul(ps[bank][:], k.lw[name][wp][:, i * P:(i + 1) * P], hs[hp][par][:],
                                                 start=(wp + hp == 0), stop=(wp == 1))
                    m.then_inc(proj, 1)

                def square_sums(g, blk):
                    n = NBLK * g + blk
                    pe.wait_ge(squared, n + 1)
                    if blk == 0:
                        need(pe, resid, g - 1)
                        need(pe, v_sb, 4 * g)
                    elif blk % 2:
                        pe.wait_ge(clipped, n)
                    else:
                        pe.wait_ge(v_sb, 4 * g + blk // 2)
                    nc.tensor.matmul(ps[BS][:], k.const["headmean"][:], sq[:, blk % 2, :],
                                     start=True, stop=True).then_inc(ssq, 1)

                def values(g, par, t):
                    pe.wait_ge(clipped, NBLK * g + 2 * t + 2)
                    for wp, hp in PASSES:
                        m = nc.tensor.matmul(ps[BS][:], hs[hp][par][:, t * P:(t + 1) * P],
                                             k.lw["wqkv"][wp][:, 2 * INNER:3 * INNER], start=(wp + hp == 0), stop=(wp == 1))
                    m.then_inc(v_mm, 1)

                def maxima_scores(g, v):
                    h, s, r, b, o = where(v)
                    pe.wait_ge(qkr_r, NBLK * g + 2 * b + 2)
                    need(pe, max_r, NU * g + v)
                    if v % HALF == 0:
                        need(pe, mT_r, 2 * g + v // HALF)
                    q, key = QKr[r:r + DH, b, :], QKr[r:r + DH, NB + b, :]
                    nc.tensor.matmul(ps[BM][:, 0:2 * KW], k.const["identb"][:], k.const["mask_q"][:], start=True, stop=False)
                    nc.tensor.matmul(ps[BM][:, WIN:KW], q[:, o:o + P], key[:, o:o + P], start=False, stop=False)
                    nc.tensor.matmul(ps[BM][:, KW:2 * KW], q[:, o + P:o + SEQ], key[:, o + WIN:o + SEQ],
                                     start=False, stop=True).then_inc(s_mm, 1)

                def scores(a, par, u):
                    h, s, r, b, o = where(u)
                    bank = ps[BT + u % 2]
                    half, r2 = u // HALF, 2 * (u % HALF)
                    if u % HALF == 0:
                        pe.wait_ge(mT_r, 2 * a + half + 1)
                    if u % 4 == 0:
                        pe.wait_ge(qk_r, NBLK * a + 2 * b + 2)
                    need(pe, pt_r, NU * a + u - 1)
                    q, key = QK[par][r:r + DH, b, :], QK[par][r:r + DH, NB + b, :]
                    nc.tensor.matmul(bank[:, 0:KW + P], k.const["identb"][:], k.const["mask_k"][:], start=True, stop=False)
                    nc.tensor.matmul(bank[:, 0:KW], key[:, o:o + P], q[:, o:o + KW], start=False, stop=False)
                    nc.tensor.matmul(bank[:, KW:KW + P], key[:, o + P:o + SEQ], q[:, o + P:o + SEQ],
                                     start=False, stop=False)
                    nc.tensor.matmul(bank[:, 0:P], sel[:, r2, :], mT[half][:], start=False, stop=False)
                    nc.tensor.matmul(bank[:, P:KW], sel[:, r2 + 1, :], mT[half][:, 0:WIN], start=False, stop=False)
                    nc.tensor.matmul(bank[:, KW:KW + P], sel[:, r2 + 1, :], mT[half][:],
                                     start=False, stop=True).then_inc(st_mm, 1)

                def weighted_values(a, par, u):
                    h, s, r, b, o = where(u)
                    if u == 0:
                        pe.wait_ge(v_sb, 4 * (a + 1))
                    if s == 0:
                        need(pe, o_r, HEADS * a + h - 1)
                    pe.wait_ge(pt_r, NU * a + u + 1)
                    bank, pt = ps[BO + h % 2], PT[:, u % 2, :]
                    nc.tensor.matmul(bank[:, o:o + KW], VA[par][:, 2 * s, h, :], pt[:, 0:KW], start=True, stop=False)
                    nc.tensor.matmul(bank[:, o + P:o + KW], VA[par][:, 2 * s + 1, h, :], pt[:, KW:KW + WIN],
                                     start=False, stop=True)
                    nc.tensor.matmul(bank[:, o + KW:o + SEQ], VA[par][:, 2 * s + 1, h, :], pt[:, KW + WIN:KW + P],
                                     start=True, stop=True).then_inc(av_mm, 1)

                def turn_maxima(c, half):
                    pe.wait_ge(max_r, NU * c + HALF * (half + 1))
                    wait_alone(k, pe, hl_r, 2 * c + half + 1)
                    nc.tensor.transpose(ps[BM][:].bitcast(BF16)[:, 0:P], hl[half][:], k.const["identb"][:]).then_inc(mT_mm, 1)

                def output(c, projected):
                    need(pe, v_sb, 4 * (c + 1 + projected))
                    pe.wait_ge(o_r, HEADS * (c + 1))
                    pe.wait_ge(w_in, L * 16 * len(names))
                    for b in range(NB):
                        i = nc.tensor.matmul(ps[BS][:], w["wo2"][:, b, :], OT[:, b, :], start=(b == 0), stop=(b == NB - 1))
                    i.then_inc(x_mm, 1)

                def step(g, par, project, attend, finish):
                    a, ap = g - 1, 1 - par
                    for blk in range(NBLK):
                        for i in range(2):
                            if project and i == 0:
                                project_block(g, par, blk)
                            if finish and blk == 0 and i == 0:
                                weighted_values(g - 2, par, NU - 1)
                            if attend and blk == EARLY and i == 0:
                                turn_maxima(a, 1)
                            if project and blk == LATE and i == 0:
                                turn_maxima(g, 0)
                            if attend:
                                u = 2 * blk + i
                                scores(a, ap, u)
                                if u > 0:
                                    weighted_values(a, ap, u - 1)
                            if project and blk >= EARLY:
                                maxima_scores(g, 2 * (blk - EARLY) + i)
                            if attend and blk < EARLY:
                                maxima_scores(a, 2 * (blk - EARLY) + NU + i)
                            if finish and blk == 0 and i == 1:
                                output(g - 2, project)
                            if project and i == (blk == 0):
                                square_sums(g, blk)
                        if project and blk % 2:
                            values(g, par, blk // 2)
                    if not project:
                        weighted_values(a, ap, NU - 1)
                        output(a, False)

                steps(pe, step)

            @block.scalar
            def _(act):
                nc.scalar.preload_act_table_set(LNEXP)
                act.wait_ge(zeroed, 4 * L)
                act.wait_ge(made, 5 * L)

                def maxima_rows(c, half):
                    act.wait_ge(mT_mm, 2 * c + half + 1)
                    nc.scalar.activation(mT[half][:], ps[BM][:].bitcast(BF16)[:, 0:P], ACT.Copy).then_inc(mT_r, 1)

                def weights(a, u):
                    act.wait_ge(st_mm, NU * a + u + 1)
                    need(act, av_mm, NU * a + u - 1)
                    nc.scalar.activation(PT[:, u % 2, :], ps[BT + u % 2][:, 0:KW + P], ACT.Exp,
                                         scale=QK_SCALE).then_inc(pt_r, 1)

                def denominators(a, h):
                    act.wait_ge(av_mm, NU * a + SPC * (h + 1))
                    need(act, o_r, HEADS * a + h - 1)
                    nc.scalar.activation(rd[:, h % 2, :], ps[BO + h % 2][DH:P, :], ACT.Ln).then_inc(ld_r, 1)
                    act.wait_ge(ld_r, HEADS * a + h + 1)
                    nc.scalar.activation(rd[:, h % 2, :], rd[:, h % 2, :], ACT.Exp, scale=-1.0).then_inc(rd_r, 1)

                def step(g, par, project, attend, finish):
                    a = g - 1
                    for blk in range(NBLK):
                        n = NBLK * g + blk
                        if project:
                            act.wait_ge(proj, n + 1)
                            need(act, ssq, n - 1)
                            nc.scalar.activation(sq[:, blk % 2, :], ps[BA][:], ACT.Square).then_inc(squared, 1)
                        if attend and blk == EARLY:
                            maxima_rows(a, 1)
                        if project and blk == LATE:
                            maxima_rows(g, 0)
                        if attend:
                            weights(a, 2 * blk)
                            if blk > 0:
                                denominators(a, blk - 1)
                            elif finish:
                                denominators(g - 2, HEADS - 1)
                            weights(a, 2 * blk + 1)
                        if project:
                            act.wait_ge(clipped, n + 1)
                            nc.scalar.activation(cl[:, blk % 2, :], cl[:, blk % 2, :], ACT.Ln,
                                                 scale=float(2 ** LN_SHIFT)).then_inc(logged, 1)
                            act.wait_ge(logged, n + 1)
                            need(act, qk_r, n - 1)
                            nc.scalar.activation(rn[:, blk % 2, :], cl[:, blk % 2, :], ACT.Exp, scale=-0.5,
                                                 bias=lnb[:, 0:1]).then_inc(rnorm, 1)
                            if blk % 2:
                                t = blk // 2
                                act.wait_ge(v_mm, 4 * g + t + 1)
                                if t == 0:
                                    need(act, av_mm, NU * (g - 1))
                                nc.scalar.activation(VA[par][:, t, :, 0:DH], ps[BS][:].rearrange("p (h d) -> p h d", d=DH),
                                                     ACT.Copy).then_inc(v_sb, 1)
                    if not project:
                        denominators(a, HEADS - 1)

                steps(act, step)

            @block.vector
            def _(dve):
                nc.vector.memset(lnb[:], 0.5 * LN_SHIFT * 0.6931471805599453).then_inc(made, 1)
                for part in hs:
                    for t in part:
                        nc.vector.tensor_scalar(t[:], k.H[:, T:T + CH], 1.0, None, ALU.mult).then_inc(made, 1)
                dve.wait_ge(made, 5 * L)

                def shift_chunk(g, par):
                    hi, lo = hs[0][par], hs[1][par]
                    early_rows, late_rows = shifted_views(k, here(g))
                    nc.vector.tensor_scalar(hi[0:DH, :], early_rows, 1.0, None, ALU.mult)
                    nc.vector.tensor_scalar(later(hi[DH:P, :]), late_rows, 1.0, None, ALU.mult).then_inc(hs_hi, 1)
                    dve.wait_ge(hs_hi, g + 1 + l)
                    nc.vector.tensor_tensor(lo[0:DH, :], early_rows, hi[0:DH, :].bitcast(F32), ALU.subtract)
                    nc.vector.tensor_tensor(later(lo[DH:P, :]), late_rows, later(hi[DH:P, :]).bitcast(F32),
                                            ALU.subtract).then_inc(shifted, 1)

                shift_chunk(G0, 0)
                dve.wait_ge(zeroed, 4 * L)

                def rounded(g, par, blk):
                    dve.wait_ge(qk_r, NBLK * g + blk + 1)
                    if blk % 2 == 0:
                        need(dve, s_mm, NU * (g - 1) + 2 * blk + 4)
                    nc.vector.tensor_scalar(QKr[:, col(blk), :], QK[par][:, col(blk), :], 1.0, None,
                                            ALU.mult).then_inc(qkr_r, 1)

                def rotate(g, blk):
                    n, t = NBLK * g + blk, 2 * (blk % 2)
                    dve.wait_ge(proj, n + 1)
                    need(dve, qk_r, n - 1)
                    nc.vector.tensor_tensor(rb[:, blk % 2, :], ps[BB][:], tab[:, t + 1, :], ALU.mult)
                    dve.wait_ge(squared, n + 1)
                    nc.vector.tensor_tensor(ra[:, blk % 2, :], ps[BA][:], tab[:, t, :], ALU.mult).then_inc(rotated, 1)

                def maximum(g, v):
                    dve.wait_ge(s_mm, NU * g + v + 1)
                    if v % HALF == 0:
                        need(dve, hl_r, 2 * g - 1 + v // HALF)
                    nc.vector.tensor_reduce(nm[:, 2 * v:2 * v + 2],
                                            ps[BM][:, 0:2 * KW].rearrange("p (a b) -> p a b", a=2),
                                            AX.X, ALU.max, negate=True).then_inc(max_r, 1)

                def normalise(a, h):
                    r = DH * (h % 2)
                    dve.wait_ge(rd_r, HEADS * a + h + 1)
                    if h == 0:
                        need(dve, x_mm, a)
                    nc.vector.tensor_tensor(OT[r:r + DH, h // 2, :], ps[BO + h % 2][0:DH, :], rd[:, h % 2, :],
                                            ALU.mult).then_inc(o_r, 1)

                def add_output(c):
                    dve.wait_ge(x_mm, c + 1)
                    nc.vector.tensor_tensor(k.H[:, here(c)], ps[BS][:], k.H[:, here(c)], ALU.add).then_inc(resid, 1)

                def clip(g, blk):
                    n = NBLK * g + blk
                    dve.wait_ge(ssq, n + 1)
                    need(dve, rnorm, n - 1)
                    nc.vector.tensor_scalar(cl[:, blk % 2, :], ps[BS][:], CLIP2, None, ALU.max).then_inc(clipped, 1)

                def split_maxima(c, half):
                    m, cols = 2 * c + half, slice(half * NU, (half + 1) * NU)
                    dve.wait_ge(max_r, NU * c + HALF * (half + 1))
                    need(dve, mT_mm, m - 1)
                    nc.vector.tensor_copy(hl[half][:, 0:NU], nm[:, cols]).then_inc(hi_r, 1)
                    dve.wait_ge(hi_r, m + 1)
                    nc.vector.tensor_tensor(hl[half][:, NU:2 * NU], nm[:, cols], hl[half][:, 0:NU], ALU.subtract).then_inc(hl_r, 1)

                def step(g, par, project, attend, finish):
                    a, ap = g - 1, 1 - par
                    for blk in range(NBLK):
                        if project and blk >= 2:
                            rounded(g, par, blk - 2)
                        if attend and blk == 1:
                            rounded(a, ap, NBLK - 2)
                            rounded(a, ap, NBLK - 1)
                        if project:
                            rotate(g, blk)
                        for i in range(2):
                            if project and blk >= EARLY:
                                maximum(g, 2 * (blk - EARLY) + i)
                            if attend and blk < EARLY:
                                maximum(a, 2 * (blk - EARLY) + NU + i)
                            if i == 0 and attend and blk > 0:
                                normalise(a, blk - 1)
                            if i == 0 and finish and blk == 0:
                                normalise(g - 2, HEADS - 1)
                            if i == 1 and finish and blk == 0:
                                add_output(g - 2)
                            if project and i == (blk == 0):
                                clip(g, blk)
                        if attend and blk == EARLY - 1:
                            split_maxima(a, 1)
                        if project and blk == LATE - 1:
                            split_maxima(g, 0)
                            need(dve, v_mm, 4 * g)
                            shift_chunk(g + 1, 1 - par)
                    if not project:
                        normalise(a, HEADS - 1)
                        add_output(a)

                steps(dve, step)

        with ExitStack() as ctx:
            W = 2
            hs = [k.sb(f"hsf{l}_{i}", [P, CH], ctx=ctx) for i in range(W)]
            hn = [k.sb(f"hn{l}_{i}", [P, CH], ctx=ctx) for i in range(W)]
            Gg = [k.sb(f"Gg{l}_{i}", [P, NHB, CH], ctx=ctx) for i in range(W)]
            U = [k.sb(f"Uf{l}_{i}", [P, NHB, CH], ctx=ctx) for i in range(W)]
            b = [ln_buffers(k, ctx, f"nf{l}_{i}", 4 * i, 4 * i + 1) for i in range(W)]
            s = LnSems(*(shared(f"nf_{n}") for n in LnSems._fields))
            sem = shared
            zeroed, shifted, affine, g_mm, a_mm, gelu, u_r, x_mm, resid = map(sem, (
                "zeroedf", "shiftedf", "affinef", "g_mm", "a_mm", "geluf", "u_r", "xf_mm", "residf"))
            raw = raw_buffers(k, l + 1, ctx) if l + 1 < DEPTH else None
            g_bank = lambda i, j: ps[4 * i + (0 if j == 1 else 2)]
            a_bank = lambda i, j: ps[4 * i + (1 if j == 1 else 3)]
            block = ctx.enter_context(nc.Block())

            @block.gpsimd
            def _(pool):
                for i in range(W):
                    nc.gpsimd.memset(hs[i][:], 0.0).then_inc(zeroed, 1)
                if raw:
                    prepare_split(k, l + 1, raw, pool)

            @block.sync
            def _(sp):
                if raw:
                    prepare_loads(k, l + 1, raw, sp)

            @block.tensor
            def _(pe):
                with pe.Fori(G0 // W, G1 // W) as c2:
                    for i in range(W):
                        c = W * c2 + i
                        pe.wait_ge(shifted, c + 1)
                        pe.wait_ge(resid, c + 1)
                        ln_centre(k, pe, s, b[i], c + 1, hs[i][:])
                    for i in range(W):
                        ln_variance(k, pe, s, b[i], W * c2 + i + 1)
                    for i in range(W):
                        c = W * c2 + i
                        pe.wait_ge(affine, c + 1)
                        for j in range(NHB):
                            n = hid_rows(j)
                            if j == 2:
                                pe.wait_ge(u_r, NHB * c + 1)
                            nc.tensor.matmul(g_bank(i, j)[0:n, :], w["w1f"][:, HID + j * P:HID + j * P + n], hn[i][:],
                                             start=True, stop=True).then_inc(g_mm, 1)
                            nc.tensor.matmul(a_bank(i, j)[0:n, :], w["w1f"][:, j * P:j * P + n], hn[i][:],
                                             start=True, stop=True).then_inc(a_mm, 1)
                    for i in range(W):
                        c = W * c2 + i
                        pe.wait_ge(u_r, NHB * (c + 1))
                        for j in range(NHB):
                            n = hid_rows(j)
                            o = nc.tensor.matmul(ps[4 * i][:], w["w2f"][0:n, j, :], U[i][0:n, j, :],
                                                 start=(j == 0), stop=(j == NHB - 1))
                        o.then_inc(x_mm, 1)

            @block.scalar
            def _(act):
                with act.Fori(G0 // W, G1 // W) as c2:
                    nc.scalar.preload_act_table_set(LNEXP)
                    for i in range(W):
                        ln_square(k, act, s, b[i], W * c2 + i + 1)
                    for i in range(W):
                        ln_rstd(k, act, s, b[i], W * c2 + i + 1)
                    for i in range(W):
                        c = W * c2 + i
                        for j in range(NHB):
                            n = hid_rows(j)
                            act.wait_ge(g_mm, NHB * c + j + 1)
                            nc.scalar.activation(Gg[i][0:n, j, :], g_bank(i, j)[0:n, :], ACT.Gelu,
                                                 bias=w["vec2"][0:n, V_B1G + j:V_B1G + j + 1]).then_inc(gelu, 1)

            @block.vector
            def _(dve):
                if l == 0:
                    dve.sem_inc(s.normed, W)
                    dve.sem_inc(resid, W)
                dve.wait_ge(zeroed, L * W)
                with dve.Fori(G0 // W, G1 // W) as c2:
                    for i in range(W):
                        shift_tokens(k, shifted, hs[i], here(W * c2 + i))
                    for i in range(W):
                        c = W * c2 + i
                        ln_scale(k, dve, s, b[i], c + 1, hn[i][:])
                        dve.wait_ge(s.normed, c + 1 + W)
                        nc.vector.tensor_scalar(hn[i][:], hn[i][:], w["vec2"][:, V_LG:V_LG + 1], w["vec2"][:, V_LB:V_LB + 1],
                                                ALU.mult, ALU.add).then_inc(affine, 1)
                    for i in range(W):
                        c = W * c2 + i
                        for j in range(NHB):
                            n = hid_rows(j)
                            dve.wait_ge(a_mm, NHB * c + j + 1)
                            dve.wait_ge(gelu, NHB * c + j + 1)
                            nc.vector.scalar_tensor_tensor(U[i][0:n, j, :], a_bank(i, j)[0:n, :],
                                                           w["vec2"][0:n, V_B1A + j:V_B1A + j + 1],
                                                           Gg[i][0:n, j, :], ALU.add, ALU.mult).then_inc(u_r, 1)
                    for i in range(W):
                        c = W * c2 + i
                        dve.wait_ge(x_mm, c + 1)
                        nc.vector.scalar_tensor_tensor(k.H[:, here(c)], ps[4 * i][:], w["vec2"][:, V_B2:V_B2 + 1],
                                                       k.H[:, here(c)], ALU.add, ALU.add).then_inc(resid, 1)


def build(nc, dram, out):
    with ExitStack() as ctx:
        k = Kernel(nc, dram, out, ctx)
        residents(k)
        norm_sems = ln_sems(nc, ctx, "norm")
        with ExitStack() as first:
            w0 = {n: k.sb(n, list(dram[n].shape), F32, first) for n in WEIGHTS0}
            load(k)
            norm_stage(k, "n0", 0, norm_sems, w0)
            linear_attention(k, w0)
        experts(k)
        sems = {}

        def shared(name):
            if name not in sems:
                sems[name] = ctx.enter_context(nc.semaphore(name))
            return sems[name]

        layer_buffers(k, shared)
        retention(k)
        norm_stage(k, "n4", NCH, norm_sems)
        for l in range(DEPTH):
            local_layer(k, l, shared)
        store(k)


def constants():
    import numpy as np

    f, bf = np.float32, np.dtype("bfloat16")
    eye = np.eye(P, dtype=f)
    c = {"ident": eye, "centre": eye - f(1 / P), "mean": np.full((P, P), 1 / P, f), "identb": eye.astype(bf)}
    c["headmean"] = np.kron(np.eye(P // DH), np.ones((DH, DH))).astype(f)
    i = np.arange(P)[:, None]
    low = -1e30
    j = np.arange(KW)[None, :]
    q0 = (j - WIN >= 0) & (j - WIN <= i) & (j - WIN >= i - WIN)
    q1 = (WIN + j <= P + i) & (WIN + j >= P + i - WIN)
    c["mask_q"] = np.where(np.concatenate([q0, q1], 1), 0, low).astype(bf)
    k0 = (i <= j) & (j <= i + WIN)
    c["mask_k"] = np.where(np.concatenate([k0, k0[:, :P]], 1), 0, low).astype(bf)
    rows = np.zeros((P, NU, P), f)
    for r in range(NU):
        rows[r, r] = rows[NU + r, r] = 1
    c["rowsel"] = rows.astype(bf)
    half = D0 // 2
    inv = f(1) / np.power(f(10000), np.arange(half, dtype=f) / f(half))
    fr = np.arange(SEQ, dtype=f)[:, None] * inv
    d = np.arange(P) % D0
    cos, sin = np.cos(fr).astype(f)[:, d % half].T, np.sin(fr).astype(f)[:, d % half].T
    sin = sin * np.where(d < half, -1, 1).astype(f)[:, None]
    c["rope0"] = np.stack([np.tile(cos, SPC), np.tile(sin, SPC)], 1)
    spread = np.zeros((P, D0, P), f)
    for dd in range(D0):
        for o in range(P):
            spread[o // D0 * D0 + dd, dd, o] = 1
    c["spread"] = spread
    c["headsum"] = np.kron(np.eye(NH0), np.ones((D0, D0))).astype(f)
    c["iota8"] = np.tile(np.arange(NE, dtype=f) - NE, (P, NT, 1))
    c["tri"] = np.triu(np.ones((P, P))).astype(bf)
    c["ones"] = np.ones((P, P), bf)
    pick = np.zeros((P, NX, P), f)
    for e in range(NX):
        pick[e:NPART * NX:NX, e] = 1
    c["pick"] = pick.reshape(P, NX * P).astype(bf)
    hi = np.arange(0, DH, 2, dtype=f)
    inv = f(1) / np.power(f(10000), hi / f(DH))
    t = np.arange(SEQ, dtype=f)
    fr = t[:, None] * inv[None, :]
    base = (hi + f(0.4 * DH)) / f(1.4 * DH)
    scale = np.power(base[None, :], ((t - SEQ // 2) / f(WIN // 2))[:, None])
    d = np.arange(P) % DH
    cs, sn, sc = (a[:, d % (DH // 2)].T.astype(f) for a in (np.cos(fr), np.sin(fr), scale))
    sn = sn * np.where(d < DH // 2, -1, 1).astype(f)[:, None]
    c["xpos"] = np.stack([np.tile(a, SPC) for a in (cs * sc, sn * sc, cs / sc, sn / sc)], 1).astype(f)
    return {n: np.ascontiguousarray(a) for n, a in c.items()}


def layouts(a):
    import numpy as np

    g = {n: np.asarray(v) for n, v in a.items()}
    r = {"x": g["L0_attn_x"]}
    o = np.arange(P)
    swap0 = o // D0 * D0 + (o % D0 + D0 // 2) % D0
    for n, s in (("q", "L0_attn_Wq"), ("k", "L0_attn_Wk")):
        r[f"w{n}0"] = g[s].T
        r[f"w{n}0s"] = g[s][swap0].T
    r["wv0"] = g["L0_attn_Wv"].T
    per_row = lambda v, m: v[o // D0 * M0 + m]
    r["wbeta"] = np.stack([per_row(g["L0_attn_Wbeta"], m).T for m in range(M0)], 1)
    r["wmix"] = np.stack([per_row(g["L0_attn_Wmix"], m).T for m in range(M0)], 1)
    r["wout0"] = g["L0_attn_Wout"].T
    r["vec0"] = np.stack([per_row(g[n], m) for n in ("L0_attn_bbeta", "L0_attn_bmix") for m in range(M0)]
                         + [g["L0_attn_bout"], g["L0_attn_ln_g"], g["L0_attn_ln_b"]], 1)
    r["wr"] = g["L0_ffn_Wr"].T
    add = lambda x, y: np.concatenate([x, y[None]], 0)
    r["w1e"] = add(g["L0_ffn_W1"], g["L0_ffn_fw1"]).transpose(1, 0, 2)
    r["w2e"] = add(g["L0_ffn_W2"], g["L0_ffn_fw2"]).reshape(NX, NJ, P, P).transpose(2, 0, 1, 3)
    r["b1e"] = add(g["L0_ffn_b1"], g["L0_ffn_fb1"]).reshape(NX, NJ, P).transpose(2, 0, 1)
    r["b2e"] = add(g["L0_ffn_b2"], g["L0_ffn_fb2"]).T
    for n in "qvgo":
        r[f"w{n}1"] = g[f"L1_attn_W{n}"].T
    r["vec1"] = np.stack([np.repeat(g["L1_attn_decay"], P // 16), g["L1_attn_ln_gamma"], g["L1_attn_ln_beta"]], 1)
    r["wqkv"] = g["L1_ffn_wqkv"]
    i = np.arange(2 * INNER)
    r["wqks"] = g["L1_ffn_wqkv"][:, :, i // DH * DH + (i % DH + DH // 2) % DH]
    r["wo2"] = g["L1_ffn_wo"].reshape(DEPTH, NB, P, P).transpose(0, 2, 1, 3)
    r["w1f"] = g["L1_ffn_w1"]
    pad = lambda v, n: np.concatenate([v, np.zeros((v.shape[0], n - v.shape[1]) + v.shape[2:], v.dtype)], 1)
    r["w2f"] = pad(g["L1_ffn_w2"], NHB * P).reshape(DEPTH, NHB, P, P).transpose(0, 2, 1, 3)
    cols = [g["L1_ffn_ln_g"], g["L1_ffn_ln_b"], g["L1_ffn_b2"]]
    for lo in (0, HID):
        v = pad(g["L1_ffn_b1"][:, lo:lo + HID], NHB * P)
        cols += [v[:, j * P:(j + 1) * P] for j in range(NHB)]
    d = np.arange(P) % DH
    ds = (d + DH // 2) % DH
    cols += [g["L1_ffn_q_scale"][:, d], g["L1_ffn_k_scale"][:, d], g["L1_ffn_q_scale"][:, ds], g["L1_ffn_k_scale"][:, ds]]
    r["vec2"] = np.stack(cols, 2)
    return {n: np.ascontiguousarray(v) for n, v in r.items()}


def kernel(**inputs):
    import concourse.bacc as _bacc
    from concourse.bass_utils import run_bass_kernel_spmd as _run

    nc = _bacc.Bacc("TRN2", target_bir_lowering=False, num_devices=1)
    arrays = {**constants(), **layouts(inputs)}
    dram = {n: nc.dram_tensor(f"{n}_dram", v.shape, mybir.dt.from_np(v.dtype), kind="ExternalInput").ap()
            for n, v in arrays.items()}
    out = nc.dram_tensor("out_dram", (NSEQ, SEQ, P), F32, kind="ExternalOutput").ap()
    build(nc, dram, out)
    r = _run(nc, [{f"{n}_dram": v for n, v in arrays.items()}], core_ids=[0])
    return r.results[0]["out_dram"]
```
